# Optimizing a Trainium2 kernel written in Bass

```python
import numpy as np
import jax
import jax.numpy as jnp

def _softmax(x, axis=-1):
    return jax.nn.softmax(x, axis=axis)

def _gelu(x):
    return jax.nn.gelu(x, approximate=True)

def _silu(x):
    return jax.nn.silu(x)

def _sigmoid(x):
    return jax.nn.sigmoid(x)

def _layernorm(x, axis=-1, eps=1e-05):
    m = jnp.mean(x, axis=axis, keepdims=True)
    v = jnp.var(x, axis=axis, keepdims=True)
    return (x - m) / jnp.sqrt(v + eps)

def _scatter_add(tgt, idx, src, axis=0):
    return tgt.at[idx].add(src)

def _segment_sum(src, seg, n):
    return jax.ops.segment_sum(src, seg, n)
kernel_name = 'mk_seq_postln_d1_jaxref_r8_f9eae1'

def setup_inputs(seed: int=0):
    np.random.seed(seed)
    _w = jnp.asarray

    def _L0_attn_setup():
        import jax, jax.numpy as jnp
        import numpy as np
        import math
        B, S, HID = (2, 500, 128)
        H, W, STRIDE = (16, 64, 32)
        D = HID // H
        key = jax.random.key(seed)
        ks = jax.random.split(key, 10)
        std = 0.02
        inp = {'hidden_states': jax.random.normal(ks[0], (B, S, HID), dtype=jnp.float32), 'Wq': jax.random.normal(ks[1], (HID, HID), dtype=jnp.float32) * std, 'bq': jnp.zeros((HID,), dtype=jnp.float32), 'Wk': jax.random.normal(ks[2], (HID, HID), dtype=jnp.float32) * std, 'bk': jnp.zeros((HID,), dtype=jnp.float32), 'Wv': jax.random.normal(ks[3], (HID, HID), dtype=jnp.float32) * std, 'bv': jnp.zeros((HID,), dtype=jnp.float32), 'Wo': jax.random.normal(ks[4], (HID, HID), dtype=jnp.float32) * std, 'bo': jnp.zeros((HID,), dtype=jnp.float32), 'pos_bias': jax.random.normal(ks[5], (H, W, W), dtype=jnp.float32) * std}
        return inp
    _L0_attn_in = _L0_attn_setup()

    def _L0_ffn_setup():
        import jax, jax.numpy as jnp
        import numpy as np
        TOP_K = 2
        key = jax.random.key(seed)
        k0, k1, k2, k3, k4 = jax.random.split(key, 5)
        B, S, D, H, E = (4, 256, 128, 256, 8)
        x = jax.random.normal(k0, (B, S, D), dtype=jnp.float32)
        router_w = jax.random.normal(k1, (E, D), dtype=jnp.float32) * D ** (-0.5)
        w_gate = jax.random.normal(k2, (E, D, H), dtype=jnp.float32) * D ** (-0.5)
        w_up = jax.random.normal(k3, (E, D, H), dtype=jnp.float32) * D ** (-0.5)
        w_down = jax.random.normal(k4, (E, H, D), dtype=jnp.float32) * H ** (-0.5)
        return {'x': x, 'router_w': router_w, 'w_gate': w_gate, 'w_up': w_up, 'w_down': w_down}
    _L0_ffn_in = _L0_ffn_setup()
    _d = {'L0_attn_hidden_states': _L0_attn_in['hidden_states'], 'L0_attn_Wq': _L0_attn_in['Wq'], 'L0_attn_bq': _L0_attn_in['bq'], 'L0_attn_Wk': _L0_attn_in['Wk'], 'L0_attn_bk': _L0_attn_in['bk'], 'L0_attn_Wv': _L0_attn_in['Wv'], 'L0_attn_bv': _L0_attn_in['bv'], 'L0_attn_Wo': _L0_attn_in['Wo'], 'L0_attn_bo': _L0_attn_in['bo'], 'L0_attn_pos_bias': _L0_attn_in['pos_bias'], 'L0_ffn_router_w': _L0_ffn_in['router_w'], 'L0_ffn_w_gate': _L0_ffn_in['w_gate'], 'L0_ffn_w_up': _L0_ffn_in['w_up'], 'L0_ffn_w_down': _L0_ffn_in['w_down']}
    _x0 = _d['L0_attn_hidden_states']
    _d['L0_attn_hidden_states'] = jax.random.normal(jax.random.fold_in(jax.random.key(seed), 1), (32, 256, 128), dtype=_x0.dtype)
    del _x0
    return _d

def reference(L0_attn_hidden_states, L0_attn_Wq, L0_attn_bq, L0_attn_Wk, L0_attn_bk, L0_attn_Wv, L0_attn_bv, L0_attn_Wo, L0_attn_bo, L0_attn_pos_bias, L0_ffn_router_w, L0_ffn_w_gate, L0_ffn_w_up, L0_ffn_w_down):

    def _L0_attn_ref(hidden_states, Wq, bq, Wk, bk, Wv, bv, Wo, bo, pos_bias):
        import jax, jax.numpy as jnp
        import numpy as np
        import math
        B, S, HID = (2, 500, 128)
        H, W, STRIDE = (16, 64, 32)
        D = HID // H
        Bb, Ss, Hid = hidden_states.shape
        scale = 1.0 / math.sqrt(D)

        def split_heads(x):
            return x.reshape(Bb, Ss, H, D).transpose(0, 2, 1, 3)
        q = split_heads(hidden_states @ Wq + bq)
        k = split_heads(hidden_states @ Wk + bk)
        v = split_heads(hidden_states @ Wv + bv)
        n_win = (Ss - W) // STRIDE + 1
        starts = jnp.arange(n_win) * STRIDE
        idx = starts[:, None] + jnp.arange(W)
        qw = q[:, :, idx]
        kw = k[:, :, idx]
        vw = v[:, :, idx]
        scores = jnp.einsum('bhnqd,bhnkd->bhnqk', qw, kw) * scale + pos_bias[None, :, None]
        probs = jax.nn.softmax(scores, axis=-1)
        ow = jnp.einsum('bhnqk,bhnkd->bhnqd', probs, vw)
        flat = idx.reshape(-1)
        merged = jnp.zeros((Bb, H, Ss, D), dtype=ow.dtype).at[:, :, flat].add(ow.reshape(Bb, H, -1, D))
        counts = jnp.zeros((Ss,), dtype=jnp.float32).at[flat].add(1.0)
        ls = Ss - W
        qt, kt, vt = (q[:, :, ls:], k[:, :, ls:], v[:, :, ls:])
        st = jnp.einsum('bhqd,bhkd->bhqk', qt, kt) * scale + pos_bias[None]
        ot = jnp.einsum('bhqk,bhkd->bhqd', jax.nn.softmax(st, axis=-1), vt)
        merged = merged.at[:, :, ls:].add(ot)
        counts = counts.at[ls:].add(1.0)
        merged = merged / jnp.clip(counts, 1.0, None)[None, None, :, None]
        ctx = merged.transpose(0, 2, 1, 3).reshape(Bb, Ss, Hid)
        return ctx @ Wo + bo

    def _L0_ffn_ref(x, router_w, w_gate, w_up, w_down):
        import jax, jax.numpy as jnp
        import numpy as np
        TOP_K = 2
        B, S, D = x.shape
        E = router_w.shape[0]
        xt = x.reshape(-1, D)
        logits = xt @ router_w.T
        topk_vals, topk_idx = jax.lax.top_k(logits, TOP_K)
        g = jax.nn.sigmoid(topk_vals)
        g = g / (g.sum(axis=-1, keepdims=True) + 1e-10)
        out = jnp.zeros_like(xt)
        for e in range(E):
            ge = jnp.sum(jnp.where(topk_idx == e, g, jnp.zeros_like(g)), axis=-1)
            h = jax.nn.silu(xt @ w_gate[e]) * (xt @ w_up[e])
            out = out + ge[:, None] * (h @ w_down[e])
        return out.reshape(B, S, D)
    x = L0_attn_hidden_states
    x = _layernorm(x + _L0_attn_ref(x, L0_attn_Wq, L0_attn_bq, L0_attn_Wk, L0_attn_bk, L0_attn_Wv, L0_attn_bv, L0_attn_Wo, L0_attn_bo, L0_attn_pos_bias), axis=-1)
    x = _layernorm(x + _L0_ffn_ref(x, L0_ffn_router_w, L0_ffn_w_gate, L0_ffn_w_up, L0_ffn_w_down), axis=-1)
    return x

_drawn_inputs = setup_inputs


def setup_inputs(seed=0):
    import zlib

    import numpy as np

    out = dict(_drawn_inputs(seed))
    spreads = {'L0_attn_bq': (0.0, 0.8),
     'L0_attn_bk': (0.0, 2.0),
     'L0_attn_bv': (0.0, 0.1),
     'L0_attn_bo': (0.0, 0.1)}
    factors = {'L0_attn_Wq': 7.716, 'L0_attn_Wk': 7.525, 'L0_attn_pos_bias': 26.638}
    for name, (base, spread) in spreads.items():
        noise = np.random.default_rng([zlib.crc32(name.encode()), seed]).standard_normal(out[name].shape)
        drawn = base * np.exp(spread * noise) if base else spread * noise
        out[name] = jnp.asarray(drawn.astype(out[name].dtype))
    for name, factor in factors.items():
        out[name] = (out[name] * factor).astype(out[name].dtype)
    return out
```

```python
from contextlib import ExitStack

import concourse.bass as bass
from concourse import mybir

F32 = mybir.dt.float32
F16 = mybir.dt.float16
BF16 = mybir.dt.bfloat16
U32 = mybir.dt.uint32
ALU = mybir.AluOpType
ACT = mybir.ActivationFunctionType
AX_X = mybir.AxisListType.X

P = 128
B, S, DM = 32, 256, 128
H, W, STRIDE = 16, 64, 32
D = DM // H
E, HID = 8, 256
EPS = 1e-5
SCALE = 1.0 / float(D) ** 0.5

STEPS = B // 2
TOK = 2 * S
TT = TOK // P
G = 4
C = 4
UNITS = [(0, 64), (128, 192), (256, 320), (384, 448), (32, 96), (288, 352), (160, 416)]
NU = len(UNITS)
SHARES = [(1.0, 0.5), (0.5, 0.5), (0.5, 1.0 / 3.0), (2.0 / 3.0, 1.0)]
TURNS = NU + 2
AHEAD = {5: [0], 6: [1, 2], 7: [3, 4], 8: [5, 6]}


def share(first_token):
    w = (first_token % S) // STRIDE
    return 0 if w == 0 else 3 if w == 6 else 2 if w == 5 else 1


def place(j, g):
    return (j % 2) * 8 + (j // 2) * 4 + g


def build(nc, x, wq, bq, wk, bk, wv, bv, wo, bo, bias, bias_t, rw_t, wg, wu, wd, out):
    NT = B * S // P
    x1_dram = nc.dram_tensor("x1_dram", (B * S, DM), F32, kind="Internal").ap()
    scratch = nc.dram_tensor("scratch", (2, 2, 4, C, D * G, TOK), F16, kind="Internal").ap()
    x_steps = x.rearrange("b s d -> (b s) d").rearrange("(i t p) d -> i p t d", t=TT, p=P)
    x1_steps = x1_dram.rearrange("(i t p) d -> i p t d", t=TT, p=P)
    x1_tiles = x1_dram.rearrange("(t p) d -> t p d", p=P)
    out_tiles = out.rearrange("b s d -> (b s) d").rearrange("(t p) d -> t p d", p=P)

    with ExitStack() as ctx:
        def sb(name, shape, dt=F32):
            return ctx.enter_context(nc.sbuf_tensor(name, shape, dt))

        def sem(name):
            return ctx.enter_context(nc.semaphore(name))

        bank = [ctx.enter_context(nc.psum_tensor(f"bank{i}", [P, 512], F32)) for i in range(2)]
        score_ps = ctx.enter_context(nc.psum_tensor("score_ps", [P, 2, 512], F32))
        scoret_ps = ctx.enter_context(nc.psum_tensor("scoret_ps", [P, 2, 512], F32))
        o_ps = ctx.enter_context(nc.psum_tensor("o_ps", [P, 512], F32))
        ctx_ps = ctx.enter_context(nc.psum_tensor("ctx_ps", [P, 512], F32))

        ident = sb("ident", [P, P])
        fold_f = sb("fold_f", [P, P])
        fold = sb("fold", [P, P], F16)
        half = sb("half", [2, P], BF16)
        diag = sb("diag", [P, 4, 64])
        minus_half = sb("minus_half", [P, TT])
        w_q, w_k, w_v, w_o = (sb(n, [P, P]) for n in ("w_q", "w_k", "w_v", "w_o"))
        b_q, b_k, b_v, b_qs = (sb(n, [P, 1]) for n in ("b_q", "b_k", "b_v", "b_qs"))
        b_o = sb("b_o", [P, P])
        bias_f = sb("bias_f", [P, 2, 1024])
        bias_hl = sb("bias_hl", [P, 2, 1024], F16)

        x_sb = sb("x_sb", [P, 2, TT, P])
        xb_sb = sb("xb_sb", [P, 2, TT, P])
        xt_sb = sb("xt_sb", [P, TOK])
        qk_f = sb("qk_f", [P, 2, TOK])
        qk_hl = sb("qk_hl", [P, 2, 2, TOK], F16)
        stack = sb("stack", [P, 2, 2, G, TOK], F16)
        v_sb = sb("v_sb", [P, 2, NU, H, 2, D + 1])
        neg_max = sb("neg_max", [P, 2, NU, H])
        maxt_sb = sb("maxt_sb", [NU * H, P], BF16)
        max_rows = sb("max_rows", [2, 2, NU * H, 64], BF16)
        prob = sb("prob", [P, 2, 1024])
        recip = sb("recip", [P, 8, 2])
        o_sb = sb("o_sb", [P, 2, 2, 8, D])
        ctxt_sb = sb("ctxt_sb", [P, TOK])
        res = sb("res", [P, TT, P])
        stats = sb("stats", [P, TT, 6])
        mean_var = sb("mean_var", [P, TT, 2])
        ve = sb("ve", [P, TT])
        rstd = sb("rstd", [P, TT])
        x1_sb = sb("x1_sb", [P, 2, TT, P])

        consts_in = sem("consts_in")
        bias_in = sem("bias_in")
        made = sem("made")
        constants = sem("constants")
        bqs_ready = sem("bqs_ready")
        dve_made = sem("dve_made")
        x_in = sem("x_in")
        xt_ps = sem("xt_ps")
        xt_ready = sem("xt_ready")
        proj_ps = sem("proj_ps")
        proj_sb = sem("proj_sb")
        halves = sem("halves")
        xb_ready = sem("xb_ready")
        scratched = sem("scratched")
        stacked = sem("stacked")
        s_half, st_half = sem("s_half"), sem("st_half")
        s_ready, max_done = sem("s_ready"), sem("max_done")
        maxt_ps, maxt_ready, rows_in = sem("maxt_ps"), sem("maxt_ready"), sem("rows_in")
        st_ready, exp_done, pv_done = sem("st_ready"), sem("exp_done"), sem("pv_done")
        recip_done, norm_done = sem("recip_done"), sem("norm_done")
        ctx_done, ctxt_ready, wo_ps = sem("ctx_done"), sem("ctxt_ready"), sem("wo_ps")
        res_done, stats_done, mv_done = sem("res_done"), sem("stats_done"), sem("mv_done")
        ve_done, rstd_done, x1_done, x1_out = sem("ve_done"), sem("rstd_done"), sem("x1_done"), sem("x1_out")

        N_CONST = 8

        def after(eng, semaphore, count):
            if not isinstance(count, int) or count > 0:
                eng.wait_ge(semaphore, count)

        def settle(eng):
            eng.nop(nofuse=True)

        def all_steps(eng, step):
            step(0, 0, True, False)
            step(1, 1, False, False)
            with eng.Fori(1, STEPS // 2 - 1) as t:
                step(2 * t, 0, False, False)
                step(2 * t + 1, 1, False, False)
            step(STEPS - 2, 0, False, False)
            step(STEPS - 1, 1, False, True)

        with nc.Block() as block:
            @block.sync
            def _(sp):
                for dst, src in ((w_q, wq), (w_k, wk), (w_v, wv), (w_o, wo)):
                    sp.dma_start(dst[:, :], src).then_inc(consts_in, 16)
                for dst, src in ((b_q, bq), (b_k, bk), (b_v, bv)):
                    sp.dma_start(dst[:, :], src.rearrange("(p a) -> p a", a=1)).then_inc(consts_in, 16)
                sp.dma_start(b_o[:, :], bo.rearrange("(a d) -> a d", a=1).to_broadcast([P, DM])).then_inc(consts_in, 16)
                sp.dma_start(x_sb[:, 0, :, :], x_steps[0]).then_inc(x_in, 16)
                for n, src in ((0, bias), (1, bias_t)):
                    for rows in (0, 64):
                        sp.dma_start(bias_f[rows:rows + 64, n, :], src).then_inc(bias_in, 16)

                def stacks(k, par):
                    after(sp, stacked, 32 * k)
                    settle(sp)
                    for n in range(2):
                        sp.wait_ge(halves, 4 * k + 2 * n + 2)
                        for c in range(C):
                            part = c % 2 if n == 0 else c // 2
                            sp.dma_start(scratch[par, n, :, c, :, :], qk_hl[:, n, part, :]).then_inc(scratched, 16)
                    sp.wait_ge(scratched, 16 * 2 * C * (k + 1))
                    for n in range(2):
                        sp.dma_start(stack[:, par, n, :, :],
                                     scratch[par, n].rearrange("j c (d g) t -> (j c d) g t", g=G)).then_inc(stacked, 16)

                def rows(k, par):
                    sp.wait_ge(maxt_ready, k + 1)
                    for a in range(2):
                        sp.dma_start(max_rows[a:a + 1, par, :, :], maxt_sb[:, 64 * a:64 * a + 64]).then_inc(rows_in, 16)

                def store(k, par):
                    sp.wait_ge(x1_done, k + 1)
                    settle(sp)
                    sp.dma_start(x1_steps[k], x1_sb[:, par, :, :]).then_inc(x1_out, 16)

                def step(i, par, first, last):
                    if not last:
                        after(sp, xt_ps, i)
                        after(sp, xb_ready, i)
                        settle(sp)
                        sp.dma_start(x_sb[:, 1 - par, :, :], x_steps[i + 1]).then_inc(x_in, 16)
                    if not first:
                        store(i - 1, 1 - par)
                    if not last:
                        after(sp, st_ready, NU * i)
                        settle(sp)
                        stacks(i + 1, 1 - par)
                        rows(i + 1, 1 - par)

                stacks(0, 0)
                rows(0, 0)
                all_steps(sp, step)
                store(STEPS - 1, 1)
                sp.wait_ge(x1_out, 16 * STEPS)

            @block.gpsimd
            def _(pool):
                count = [0]

                def link(ins):
                    count[0] += 1
                    ins.then_inc(made, 1)
                    pool.wait_ge(made, count[0])

                link(pool.memset(ident[:, :], 0.0))
                link(pool.affine_select(out=ident[:, :], in_=ident[:, :], compare_op=ALU.not_equal, fill=1.0, base=0,
                                        pattern=[[-1, P]], channel_multiplier=1))
                link(pool.memset(fold_f[:, :], 0.0))
                for base in (0, 64, -64):
                    link(pool.affine_select(out=fold_f[:, :], in_=fold_f[:, :], compare_op=ALU.not_equal, fill=1.0,
                                            base=base, pattern=[[-1, P]], channel_multiplier=1))
                link(pool.tensor_copy(fold[:, :], fold_f[:, :]))
                link(pool.memset(half[:, :], 1.0))
                link(pool.affine_select(out=half[:, :], in_=half[:, :], compare_op=ALU.is_ge, fill=0.0, base=0,
                                        pattern=[[1, P]], channel_multiplier=-64))
                link(pool.affine_select(out=half[:, :], in_=half[:, :], compare_op=ALU.is_ge, fill=0.0, base=63,
                                        pattern=[[-1, P]], channel_multiplier=64))
                for n, shares in enumerate(SHARES):
                    for q in range(4):
                        link(pool.tensor_scalar(diag[32 * q:32 * q + 32, n, :], fold_f[32 * q:32 * q + 32, 0:64],
                                                shares[q % 2], None, ALU.mult))
                link(pool.memset(v_sb[:, :, :, :, :, :], 0.0))
                for a in range(2):
                    for par in range(2):
                        link(pool.memset(v_sb[64 * a:64 * a + 64, par, :, :, a, D:D + 1], 1.0))
                pool.memset(minus_half[:, :], -0.5).then_inc(constants, 1)

                def split(k, par):
                    pool.wait_ge(x_in, 16 * (k + 1))
                    after(pool, res_done, k - 1)
                    after(pool, scratched, 16 * 2 * C * k)
                    pool.tensor_tensor(xb_sb[:, par, :, :], x_sb[:, par, :, :],
                                       b_o[:, :].unsqueeze(1).to_broadcast([P, TT, P]), ALU.add).then_inc(xb_ready, 1)
                    for n in range(2):
                        pool.wait_ge(proj_sb, 4 * k + n + 1)
                        settle(pool)
                        pool.tensor_copy(qk_hl[:, n, 0, :], qk_f[:, n, :]).then_inc(halves, 1)
                        pool.wait_ge(halves, 4 * k + 2 * n + 1)
                        pool.tensor_tensor(qk_hl[:, n, 1, :], qk_f[:, n, :], qk_hl[:, n, 0, :], ALU.subtract).then_inc(halves, 1)

                def norm(k, par):
                    pool.wait_ge(mv_done, k + 1)
                    settle(pool)
                    pool.tensor_scalar(ve[:, :], mean_var[:, :, 1], EPS, None, ALU.add).then_inc(ve_done, 1)
                    pool.wait_ge(ve_done, k + 1)
                    pool.tensor_tensor(rstd[:, :], ve[:, :], minus_half[:, :], ALU.pow).then_inc(rstd_done, 1)
                    pool.wait_ge(rstd_done, k + 1)
                    after(pool, x1_out, 16 * k)
                    settle(pool)
                    for t in range(TT):
                        last = pool.tensor_scalar(x1_sb[:, par, t, :], res[:, t, :], mean_var[:, t, 0:1], rstd[:, t:t + 1],
                                                  ALU.subtract, ALU.mult)
                    last.then_inc(x1_done, 1)

                def step(i, par, first, last):
                    if not first:
                        norm(i - 1, 1 - par)
                    if not last:
                        split(i + 1, 1 - par)

                pool.wait_ge(constants, 1)
                pool.wait_ge(consts_in, 16 * N_CONST)
                split(0, 0)
                all_steps(pool, step)
                norm(STEPS - 1, 1)

            @block.scalar
            def _(act):
                act.wait_ge(consts_in, 16 * N_CONST)
                act.mul(b_qs[:, :], b_q[:, :], SCALE).then_inc(bqs_ready, 1)
                act.wait_ge(bqs_ready, 1)
                act.wait_ge(constants, 1)

                def copies(k, par):
                    act.wait_ge(xt_ps, k + 1)
                    after(act, proj_ps, 4 * k)
                    act.copy(xt_sb[:, :], bank[1][:, :]).then_inc(xt_ready, 1)
                    for n, (b, s) in enumerate(((b_qs, SCALE), (b_k, 1.0))):
                        act.wait_ge(proj_ps, 4 * k + n + 1)
                        after(act, halves, 4 * k - 2 + 2 * n)
                        act.activation(qk_f[:, n, :], bank[n][:, :], ACT.Identity, bias=b[:, :], scale=s).then_inc(proj_sb, 1)
                    for n, (u0, u1) in enumerate(((0, 4), (4, NU))):
                        act.wait_ge(proj_ps, 4 * k + n + 3)
                        after(act, pv_done, NU * (k - 1))
                        for a in range(2):
                            rows = slice(64 * a, 64 * a + 64)
                            last = act.copy(v_sb[rows, par, u0:u1, :, a, 0:D],
                                            bank[n][rows, 0:(u1 - u0) * P].rearrange("p (u h d) -> p u h d", h=H, d=D))
                        last.then_inc(proj_sb, 1)

                def ctx_copy(k):
                    act.wait_ge(ctx_done, NU * (k + 1))
                    after(act, wo_ps, k)
                    act.activation(ctxt_sb[:, :], ctx_ps[:, :], ACT.Identity, bias=b_v[:, :], scale=1.0).then_inc(ctxt_ready, 1)

                def step(i, par, first, last):
                    if not first:
                        ctx_copy(i - 1)
                    for u in range(NU):
                        act.wait_ge(st_ready, NU * i + u + 1)
                        after(act, pv_done, NU * i + u - 1)
                        act.activation(prob[:, (par + u) % 2, :], scoret_ps[:, :, :].rearrange("p b c -> p (b c)"),
                                       ACT.Exp).then_inc(exp_done, 1)
                        if u == 1 and not last:
                            copies(i + 1, 1 - par)

                copies(0, 0)
                all_steps(act, step)
                ctx_copy(STEPS - 1)

            @block.vector
            def _(dve):
                dve.wait_ge(bias_in, 64)
                dve.tensor_copy(bias_hl[:, :, :], bias_f[:, :, :]).then_inc(dve_made, 1)
                dve.wait_ge(dve_made, 1)
                dve.tensor_tensor(bias_hl[64:128, :, :], bias_f[64:128, :, :], bias_hl[64:128, :, :],
                                  ALU.subtract).then_inc(dve_made, 1)

                def maximum(k, par, v):
                    dve.wait_ge(s_ready, NU * k + v + 1)
                    dve.tensor_reduce(neg_max[:, par, v, :], score_ps[:, :, :].rearrange("p b (h k) -> p (b h) k", k=W),
                                      AX_X, ALU.max, negate=True).then_inc(max_done, 1)

                def max_copy(k):
                    dve.wait_ge(maxt_ps, k + 1)
                    after(dve, rows_in, 32 * k)
                    dve.tensor_copy(maxt_sb[:, :], bank[0][0:NU * H, 0:P]).then_inc(maxt_ready, 1)

                def normalise(i, par, u):
                    n = NU * i + u
                    dve.wait_ge(pv_done, n + 1)
                    o = o_ps[:, 0:288].rearrange("p (h e a d) -> p h e a d", h=8, e=2, a=2)
                    for e in range(2):
                        rows = slice(64 * e, 64 * e + 64)
                        dve.reciprocal(recip[rows, :, :], o[rows, :, e, :, D]).then_inc(recip_done, 1)
                    dve.wait_ge(recip_done, 2 * n + 2)
                    after(dve, ctx_done, n - 1)
                    for e in range(2):
                        rows = slice(64 * e, 64 * e + 64)
                        last = dve.tensor_tensor(o_sb[rows, (par + u) % 2, :, :, :].rearrange("p a h d -> p h a d"),
                                                 o[rows, :, e, :, 0:D],
                                                 recip[rows, :, :].unsqueeze(3).to_broadcast([64, 8, 2, D]), ALU.mult)
                    last.then_inc(norm_done, 1)

                def residual(k, par):
                    dve.wait_ge(wo_ps, k + 1)
                    dve.wait_ge(xb_ready, k + 1)
                    after(dve, x1_done, k)
                    dve.tensor_tensor(res[:, :, :], bank[0][:, :].rearrange("p (t d) -> p t d", t=TT), xb_sb[:, par, :, :],
                                      ALU.add).then_inc(res_done, 1)
                    dve.wait_ge(res_done, k + 1)
                    for t in range(TT):
                        last = dve.bn_stats(stats[:, t, :], res[:, t, :])
                    last.then_inc(stats_done, 1)
                    dve.wait_ge(stats_done, k + 1)
                    settle(dve)
                    for t in range(TT):
                        last = dve.bn_aggr(mean_var[:, t, :], stats[:, t, :])
                    last.then_inc(mv_done, 1)

                def step(i, par, first, last):
                    if not first:
                        residual(i - 1, 1 - par)
                    for u in range(TURNS):
                        if 1 <= u <= NU:
                            normalise(i, par, u - 1)
                        if not last:
                            for v in AHEAD.get(u, []):
                                maximum(i + 1, 1 - par, v)
                    if not last:
                        max_copy(i + 1)

                for v in range(NU):
                    maximum(0, 0, v)
                max_copy(0)
                all_steps(dve, step)
                residual(STEPS - 1, 1)

            @block.tensor
            def _(pe):
                pe.wait_ge(consts_in, 16 * N_CONST)
                pe.wait_ge(constants, 1)

                def project(k, par):
                    pe.wait_ge(x_in, 16 * (k + 1))
                    after(pe, proj_sb, 4 * k)
                    for t in range(TT):
                        last = pe.transpose(bank[1][:, t * P:(t + 1) * P], x_sb[:, par, t, :], ident[:, :])
                    last.then_inc(xt_ps, 1)
                    after(pe, maxt_ready, k)
                    after(pe, res_done, k - 1)
                    pe.wait_ge(xt_ready, k + 1)
                    pe.matmul(bank[0][:, :], w_q[:, :], xt_sb[:, :], start=True, stop=True).then_inc(proj_ps, 1)
                    pe.matmul(bank[1][:, :], w_k[:, :], xt_sb[:, :], start=True, stop=True).then_inc(proj_ps, 1)
                    for n, (u0, u1) in enumerate(((0, 4), (4, NU))):
                        pe.wait_ge(proj_sb, 4 * k + n + 1)
                        for u in range(u0, u1):
                            a, b = UNITS[u]
                            cols = slice((u - u0) * P, (u - u0 + 1) * P)
                            if b == a + W:
                                last = pe.matmul(bank[n][:, cols], xt_sb[:, a:a + P], w_v[:, :], start=True, stop=True)
                            else:
                                for r, t0 in ((0, a), (W, b)):
                                    last = pe.matmul(bank[n][r:r + W, cols], xt_sb[:, t0:t0 + W], w_v[:, :],
                                                     start=True, stop=True)
                        last.then_inc(proj_ps, 1)

                def products(ps, par, u, a_of, b_of, jj):
                    for g in range(G):
                        for a in range(2):
                            t0 = UNITS[u][a]
                            for j in (2 * jj, 2 * jj + 1):
                                n = place(j, g)
                                rows = slice(32 * j, 32 * j + 32)
                                last = pe.matmul(ps[64 * a:64 * a + 64, n // 8, (n % 8) * W:(n % 8 + 1) * W],
                                                 stack[rows, par, a_of, g, t0:t0 + W],
                                                 stack[rows, par, b_of, g, t0:t0 + W],
                                                 start=False, stop=(jj == 1 and g == G - 1), skip_group_check=True)
                    return last

                def scores_a(k, par, v):
                    if v == 0:
                        pe.wait_ge(stacked, 32 * (k + 1))
                    after(pe, max_done, NU * k + v)
                    for n in range(2):
                        pe.matmul(score_ps[:, n, :], fold[:, :], bias_hl[:, 0, n * 512:n * 512 + 512],
                                  start=True, stop=False, skip_group_check=True)
                    products(score_ps, par, v, 0, 1, 0).then_inc(s_half, 1)

                def scores_b(k, par, v):
                    pe.wait_ge(s_half, NU * k + v + 1)
                    products(score_ps, par, v, 0, 1, 1).then_inc(s_ready, 1)

                def scores_t_a(i, par, u):
                    if u == 0:
                        pe.wait_ge(rows_in, 32 * (i + 1))
                    after(pe, exp_done, NU * i + u)
                    for n in range(2):
                        pe.matmul(scoret_ps[:, n, :], fold[:, :], bias_hl[:, 1, n * 512:n * 512 + 512],
                                  start=True, stop=False, skip_group_check=True)
                    for n in range(2):
                        pe.matmul(scoret_ps[:, n, :], half[:, :],
                                  max_rows[:, par, u * H + 8 * n:u * H + 8 * n + 8, :].rearrange("a h q -> a (h q)"),
                                  start=False, stop=False, skip_group_check=True)
                    products(scoret_ps, par, u, 1, 0, 0).then_inc(st_half, 1)

                def scores_t_b(i, par, u):
                    pe.wait_ge(st_half, NU * i + u + 1)
                    products(scoret_ps, par, u, 1, 0, 1).then_inc(st_ready, 1)

                def values(i, par, u):
                    n = NU * i + u
                    pe.wait_ge(exp_done, n + 1)
                    if u == 0:
                        pe.wait_ge(proj_sb, 4 * (i + 1))
                    after(pe, norm_done, n)
                    for h in range(8):
                        last = pe.matmul(o_ps[:, h * 36:h * 36 + 36], prob[:, (par + u) % 2, h * P:(h + 1) * P],
                                         v_sb[:, par, u, 2 * h:2 * h + 2, :, :].rearrange("p h a d -> p (h a d)"),
                                         start=True, stop=True)
                    last.then_inc(pv_done, 1)

                def context(i, par, u):
                    pe.wait_ge(norm_done, NU * i + u + 1)
                    if u == 0:
                        after(pe, ctxt_ready, i)
                    settle(pe)
                    for a in range(2):
                        t0 = UNITS[u][a]
                        for e in range(2):
                            rows = slice(64 * e, 64 * e + 64)
                            last = pe.matmul(ctx_ps[rows, t0:t0 + W],
                                             o_sb[rows, (par + u) % 2, a, :, :].rearrange("p h d -> p (h d)"),
                                             diag[rows, share(t0), :], start=(u == 0 and a == 0), stop=(u == NU - 1),
                                             skip_group_check=True)
                    last.then_inc(ctx_done, 1)

                def project_out(k):
                    pe.wait_ge(ctxt_ready, k + 1)
                    for t in range(TT):
                        last = pe.matmul(bank[0][:, t * P:(t + 1) * P], ctxt_sb[:, t * P:(t + 1) * P], w_o[:, :],
                                         start=True, stop=True)
                    last.then_inc(wo_ps, 1)

                def turn_maxima(k, par):
                    pe.wait_ge(max_done, NU * (k + 1))
                    pe.wait_ge(proj_sb, 4 * k + 3)
                    pe.transpose(bank[0][0:NU * H, 0:P], neg_max[:, par, :, :].rearrange("p u h -> p (u h)"),
                                 ident[:, :]).then_inc(maxt_ps, 1)

                def step(i, par, first, last):
                    if not first:
                        pe.wait_ge(maxt_ready, i + 1)
                        project_out(i - 1)
                    for u in range(TURNS):
                        ahead = [] if last else AHEAD.get(u, [])
                        if u < NU:
                            scores_t_a(i, par, u)
                        if ahead:
                            scores_a(i + 1, 1 - par, ahead[0])
                        if 1 <= u <= NU:
                            values(i, par, u - 1)
                        if u < NU:
                            scores_t_b(i, par, u)
                        if ahead:
                            scores_b(i + 1, 1 - par, ahead[0])
                        if len(ahead) > 1:
                            scores_a(i + 1, 1 - par, ahead[1])
                        if u >= 2:
                            context(i, par, u - 2)
                        if len(ahead) > 1:
                            scores_b(i + 1, 1 - par, ahead[1])
                        if u == 1 and not last:
                            project(i + 1, 1 - par)
                    if not last:
                        turn_maxima(i + 1, 1 - par)

                project(0, 0)
                pe.wait_ge(dve_made, 2)
                for v in range(NU):
                    scores_a(0, 0, v)
                    scores_b(0, 0, v)
                turn_maxima(0, 0)
                all_steps(pe, step)
                project_out(STEPS - 1)

        if True:
            wgu_sb = sb("wgu_sb", [P, E, 2 * HID])
            wd_sb = sb("wd_sb", [P, E, 2, P])
            rw_sb = sb("rw_sb", [P, E])
            lane = sb("lane", [P, E])
            xin = sb("xin", [P, 2, P])
            xt2 = sb("xt2", [P, P])
            logit = sb("logit", [P, E])
            top = sb("top", [P, E])
            top_at = sb("top_at", [P, E], U32)
            top_f = sb("top_f", [P, 2])
            gate2 = sb("gate2", [P, 2])
            gsum = sb("gsum", [P, 1])
            ginv = sb("ginv", [P, 1])
            gnorm = sb("gnorm", [P, 2])
            pick = sb("pick", [P, 2, E])
            share_e = sb("share_e", [P, E])
            silu_sb = sb("silu_sb", [P, 2, HID])
            h_sb = sb("h_sb", [P, 2, HID])
            ht_sb = sb("ht_sb", [P, 2, HID])
            acc = sb("acc", [P, P])
            stats2 = sb("stats2", [P, 6])
            mv2 = sb("mv2", [P, 2])
            ve2, rstd2 = sb("ve2", [P, 1]), sb("rstd2", [P, 1])
            y_sb = sb("y_sb", [P, 2, P])
            w_in, lane_made = sem("w_in"), sem("lane_made")
            xin_in = [sem("xin_in0"), sem("xin_in1")]
            xt2_ps, xt2_ready = sem("xt2_ps"), sem("xt2_ready")
            logit_ps, chain, gates = sem("logit_ps"), sem("chain"), sem("gates")
            top_done, shares_done = sem("top_done"), sem("shares_done")
            gu_ps, silu_done, h_done = sem("gu_ps"), sem("silu_done"), sem("h_done")
            ht_ps, ht_ready, y_ps, acc_done = sem("ht_ps"), sem("ht_ready"), sem("y_ps"), sem("acc_done")
            norm2 = sem("norm2")
            mv2_done, ve2_done, rstd2_done, y_done, y_out = (sem(n) for n in ("mv2_done", "ve2_done", "rstd2_done", "y_done", "y_out"))

            def all_tiles(eng, tile):
                tile(0, 0, 0)
                tile(1, 1, 0)
                with eng.Fori(1, NT // 2 - 1) as t:
                    tile(2 * t, 0, t)
                    tile(2 * t + 1, 1, t)
                tile(NT - 2, 0, NT // 2 - 1)
                tile(NT - 1, 1, NT // 2 - 1)

            with nc.Block() as block:
                @block.sync
                def _(sp):
                    sp.dma_start(xin[:, 0, :], x1_tiles[0]).then_inc(xin_in[0], 16)
                    sp.dma_start(rw_sb[:, :], rw_t).then_inc(w_in, 16)
                    sp.dma_start(wgu_sb[:, :, 0:HID], wg.rearrange("e d h -> d e h")).then_inc(w_in, 16)
                    sp.dma_start(wgu_sb[:, :, HID:2 * HID], wu.rearrange("e d h -> d e h")).then_inc(w_in, 16)
                    sp.dma_start(wd_sb[:, :, :, :], wd.rearrange("e (n p) d -> p e n d", p=P)).then_inc(w_in, 16)

                    def tile(n, par, t):
                        if not (isinstance(n, int) and n == NT - 1):
                            after(sp, acc_done, E * n)
                            settle(sp)
                            sp.dma_start(xin[:, 1 - par, :], x1_tiles[n + 1]).then_inc(xin_in[1 - par], 16)
                        sp.wait_ge(y_done, n + 1)
                        settle(sp)
                        sp.dma_start(out_tiles[n], y_sb[:, par, :]).then_inc(y_out, 16)

                    all_tiles(sp, tile)
                    sp.wait_ge(y_out, 16 * NT)

                @block.gpsimd
                def _(pool):
                    pool.iota(lane[:, :], pattern=[[1, E]], base=0, channel_multiplier=0,
                              allow_small_or_imprecise_dtypes=True).then_inc(lane_made, 1)

                    def tile(n, par, t):
                        pool.wait_ge(mv2_done, n + 1)
                        after(pool, y_done, n)
                        settle(pool)
                        pool.tensor_scalar(ve2[:, :], mv2[:, 1:2], EPS, None, ALU.add).then_inc(ve2_done, 1)
                        pool.wait_ge(ve2_done, n + 1)
                        pool.tensor_tensor(rstd2[:, :], ve2[:, :], minus_half[:, 0:1], ALU.pow).then_inc(rstd2_done, 1)

                    all_tiles(pool, tile)

                @block.scalar
                def _(act):
                    def tile(n, par, t):
                        act.wait_ge(xt2_ps, n + 1)
                        after(act, gu_ps, E * n)
                        act.copy(xt2[:, :], bank[0][:, 0:P]).then_inc(xt2_ready, 1)
                        act.wait_ge(top_done, n + 1)
                        after(act, shares_done, n)
                        act.activation(gate2[:, :], top[:, 0:2], ACT.Sigmoid).then_inc(gates, 1)
                        for e in range(E):
                            m = E * n + e
                            act.wait_ge(gu_ps, m + 1)
                            after(act, h_done, m - 1)
                            act.activation(silu_sb[:, e % 2, :], score_ps[:, e % 2, 0:HID], ACT.Silu).then_inc(silu_done, 1)
                            if e:
                                turn(m - 1, (e - 1) % 2)
                        turn(E * n + E - 1, (E - 1) % 2)

                    def turn(m, b):
                        act.wait_ge(ht_ps, m + 1)
                        after(act, y_ps, m - 1)
                        act.copy(ht_sb[:, b, :], scoret_ps[:, b, 0:HID]).then_inc(ht_ready, 1)

                    all_tiles(act, tile)

                @block.vector
                def _(dve):
                    dve.wait_ge(lane_made, 1)
                    CH = 7

                    def tile(n, par, t):
                        dve.wait_ge(logit_ps, n + 1)
                        step = [CH * n]

                        def link(ins):
                            step[0] = step[0] + 1
                            ins.then_inc(chain, 1)
                            dve.wait_ge(chain, step[0])
                            settle(dve)

                        after(dve, gates, n)
                        link(dve.tensor_copy(logit[:, :], bank[1][:, 0:E]))
                        link(dve.max(top[:, :], logit[:, :]))
                        dve.max_index(top_at[:, :], top[:, :], logit[:, :]).then_inc(top_done, 1)
                        dve.wait_ge(top_done, n + 1)
                        link(dve.tensor_copy(top_f[:, :], top_at[:, 0:2]))
                        dve.wait_ge(gates, n + 1)
                        link(dve.tensor_scalar(gsum[:, :], gate2[:, 0:1], gate2[:, 1:2], 1e-10, ALU.add, ALU.add))
                        link(dve.reciprocal(ginv[:, :], gsum[:, :]))
                        link(dve.tensor_scalar(gnorm[:, :], gate2[:, :], ginv[:, 0:1], None, ALU.mult))
                        for c in range(2):
                            last = dve.tensor_scalar(pick[:, c, :], lane[:, :], top_f[:, c:c + 1], gnorm[:, c:c + 1],
                                                     ALU.is_equal, ALU.mult)
                        link(last)
                        dve.tensor_tensor(share_e[:, :], pick[:, 0, :], pick[:, 1, :], ALU.add).then_inc(shares_done, 1)
                        dve.wait_ge(shares_done, n + 1)
                        for e in range(E):
                            m = E * n + e
                            dve.wait_ge(silu_done, m + 1)
                            after(dve, ht_ps, m - 1)
                            dve.tensor_tensor(h_sb[:, e % 2, :], silu_sb[:, e % 2, :], score_ps[:, e % 2, HID:2 * HID],
                                              ALU.mult).then_inc(h_done, 1)
                            if e:
                                add(n, par, e - 1)
                        add(n, par, E - 1)
                        dve.bn_stats(stats2[:, :], acc[:, :]).then_inc(norm2, 1)
                        dve.wait_ge(norm2, n + 1)
                        settle(dve)
                        dve.bn_aggr(mv2[:, :], stats2[:, :]).then_inc(mv2_done, 1)
                        dve.wait_ge(rstd2_done, n + 1)
                        after(dve, y_out, 16 * n)
                        dve.tensor_scalar(y_sb[:, par, :], acc[:, :], mv2[:, 0:1], rstd2[:, 0:1], ALU.subtract,
                                          ALU.mult).then_inc(y_done, 1)
                        dve.engine_nop() if False else None
                        dve.wait_ge(y_done, n + 1)

                    def add(n, par, e):
                        m = E * n + e
                        dve.wait_ge(y_ps, m + 1)
                        after(dve, acc_done, m)
                        y = (o_ps, ctx_ps)[e % 2]
                        dve.scalar_tensor_tensor(out=acc[:, :], in0=y[:, 0:P], scalar=share_e[:, e:e + 1],
                                                 in1=acc[:, :] if e else xin[:, par, :], op0=ALU.mult,
                                                 op1=ALU.add).then_inc(acc_done, 1)
                        if e == E - 1:
                            dve.wait_ge(acc_done, m + 1)

                    all_tiles(dve, tile)

                @block.tensor
                def _(pe):
                    pe.wait_ge(w_in, 64)

                    def tile(n, par, t):
                        pe.wait_ge(xin_in[par], 16 * (t + 1))
                        pe.transpose(bank[0][:, 0:P], xin[:, par, :], ident[:, :]).then_inc(xt2_ps, 1)
                        pe.wait_ge(xt2_ready, n + 1)
                        after(pe, top_done, n)
                        pe.matmul(bank[1][:, 0:E], xt2[:, :], rw_sb[:, :], start=True, stop=True).then_inc(logit_ps, 1)
                        for e in range(E):
                            m = E * n + e
                            after(pe, h_done, m - 1)
                            pe.matmul(score_ps[:, e % 2, :], xt2[:, :], wgu_sb[:, e, :], start=True, stop=True).then_inc(gu_ps, 1)
                            if e:
                                turn(m - 1, (e - 1) % 2)
                            if e > 1:
                                down(m - 2, e - 2)
                        turn(E * n + E - 1, (E - 1) % 2)
                        down(E * n + E - 2, E - 2)
                        down(E * n + E - 1, E - 1)

                    def turn(m, b):
                        pe.wait_ge(h_done, m + 1)
                        after(pe, ht_ready, m - 1)
                        for c in range(2):
                            last = pe.transpose(scoret_ps[:, b, c * P:(c + 1) * P], h_sb[:, b, c * P:(c + 1) * P], ident[:, :])
                        last.then_inc(ht_ps, 1)

                    def down(m, e):
                        pe.wait_ge(ht_ready, m + 1)
                        after(pe, acc_done, m - 1)
                        y = (o_ps, ctx_ps)[e % 2]
                        for c in range(2):
                            last = pe.matmul(y[:, 0:P], ht_sb[:, e % 2, c * P:(c + 1) * P], wd_sb[:, e, c, :],
                                             start=(c == 0), stop=(c == 1))
                        last.then_inc(y_ps, 1)

                    all_tiles(pe, tile)


def kernel(**inputs):
    import numpy as np
    import concourse.bacc as bacc
    from concourse import mybir as mb
    from concourse.bass_utils import run_bass_kernel_spmd

    a = {n.replace("L0_attn_", "").replace("L0_ffn_", ""): np.asarray(v) for n, v in inputs.items()}
    qk = np.array([8 * (4 * g + j) + d for j in range(4) for d in range(D) for g in range(G)])
    order = np.empty(H, int)
    for j in range(4):
        for g in range(G):
            order[place(j, g)] = 4 * g + j
    vals = np.array([8 * h + d for h in order for d in range(D)])
    turned = np.array([8 * h + d for h in np.concatenate([order[0::2], order[1::2]]) for d in range(D)])
    bias = a["pos_bias"][order]
    arrays = {
        "x": a["hidden_states"], "wq": a["Wq"][:, qk], "bq": a["bq"][qk], "wk": a["Wk"][:, qk], "bk": a["bk"][qk],
        "wv": a["Wv"][:, vals], "bv": a["bv"][turned], "wo": a["Wo"][turned], "bo": a["bo"],
        "bias": bias.transpose(1, 0, 2).reshape(W, H * W), "bias_t": bias.transpose(2, 0, 1).reshape(W, H * W),
        "rw_t": a["router_w"].T, "wg": a["w_gate"], "wu": a["w_up"], "wd": a["w_down"],
    }
    nc = bacc.Bacc("TRN2", target_bir_lowering=False, num_devices=1)
    feeds, args = {}, []
    for name, v in arrays.items():
        v = np.ascontiguousarray(v)
        feeds[f"in_{name}"] = v
        args.append(nc.dram_tensor(f"in_{name}", v.shape, mb.dt.from_np(v.dtype), kind="ExternalInput").ap())
    args.append(nc.dram_tensor("out_0", (B, S, DM), mb.dt.float32, kind="ExternalOutput").ap())
    build(nc, *args)
    r = run_bass_kernel_spmd(nc, [feeds], core_ids=[0])
    return r.results[0]["out_0"]
```

```python
from contextlib import ExitStack

import concourse.bass as bass
from concourse import mybir

F32 = mybir.dt.float32
F32R = mybir.dt.float32r
F16 = mybir.dt.float16
BF16 = mybir.dt.bfloat16
U32 = mybir.dt.uint32
ALU = mybir.AluOpType
ACT = mybir.ActivationFunctionType
AX_X = mybir.AxisListType.X

P = 128
B, S, DM = 32, 256, 128
H, W, STRIDE = 16, 64, 32
D = DM // H
E, HID = 8, 256
EPS = 1e-5
EULER = 2.718281828459045
SCALE = 1.0 / float(D) ** 0.5

STEPS = B // 2
TOK = 2 * S
TT = TOK // P
CHUNKS = B * S // TOK
G = 4
C = 4
UNITS = [(0, 64), (128, 192), (256, 320), (384, 448), (32, 96), (288, 352), (160, 416)]
NU = len(UNITS)
SHARES = [(1.0, 0.5), (0.5, 0.5), (0.5, 1.0 / 3.0), (2.0 / 3.0, 1.0)]
TURNS = NU + 2


def share(first_token):
    w = (first_token % S) // STRIDE
    return 0 if w == 0 else 3 if w == 6 else 2 if w == 5 else 1


def place(j, g):
    return 4 * g + j


def build(nc, x, wq, bq, wk, bk, wv, bv, wo, bo, bias, bias_t, rw_t, wg, wu, wd, out):
    x1_dram = nc.dram_tensor("x1_dram", (B * S, DM), F32, kind="Internal").ap()
    scratch = nc.dram_tensor("scratch", (2, 2, 4, C, D * G, TOK), F16, kind="Internal").ap()
    x_steps = x.rearrange("b s d -> (b s) d").rearrange("(i t p) d -> i p t d", t=TT, p=P)
    x1_steps = x1_dram.rearrange("(i t p) d -> i p t d", t=TT, p=P)
    out_steps = out.rearrange("b s d -> (b s) d").rearrange("(i t p) d -> i p t d", t=TT, p=P)

    with ExitStack() as ctx:
        def sb(name, shape, dt=F32):
            return ctx.enter_context(nc.sbuf_tensor(name, shape, dt))

        def sem(name):
            return ctx.enter_context(nc.semaphore(name))

        bank = [ctx.enter_context(nc.psum_tensor(f"bank{i}", [P, 512], F32)) for i in range(2)]
        score_ps = ctx.enter_context(nc.psum_tensor("score_ps", [P, 2, 512], F32))
        scoret_ps = ctx.enter_context(nc.psum_tensor("scoret_ps", [P, 2, 512], F32))
        o_ps = ctx.enter_context(nc.psum_tensor("o_ps", [P, 512], F32))
        ctx_ps = ctx.enter_context(nc.psum_tensor("ctx_ps", [P, 512], F32))

        ident = sb("ident", [P, P])
        fold_f = sb("fold_f", [P, P])
        fold = sb("fold", [P, P], F16)
        half = sb("half", [P, P], BF16)
        diag = sb("diag", [P, 4, 64])
        minus_half = sb("minus_half", [P, TT])
        w_q, w_k, w_v, w_o = (sb(n, [P, P]) for n in ("w_q", "w_k", "w_v", "w_o"))
        b_q, b_k, b_v, b_qs = (sb(n, [P, 1]) for n in ("b_q", "b_k", "b_v", "b_qs"))
        b_o = sb("b_o", [P, P])
        bias_hl = sb("bias_hl", [P, 2, 1024], F16)

        wgu_sb = sb("wgu_sb", [P, E, 2 * HID])
        wd_sb = sb("wd_sb", [P, E, 2, P])
        rw_sb = sb("rw_sb", [P, E])

        attention = ExitStack()

        def sb(name, shape, dt=F32):
            return attention.enter_context(nc.sbuf_tensor(name, shape, dt))

        x_sb = sb("x_sb", [P, 2, TT, P])
        xb_sb = sb("xb_sb", [P, 2, TT, P])
        xt_sb = sb("xt_sb", [P, 2, TOK])
        qk_f = sb("qk_f", [P, 2, TOK])
        qk_hl = sb("qk_hl", [P, 2, 2, TOK], F16)
        stack = sb("stack", [P, 2, 2, G, TOK], F16)
        blocks = sb("blocks", [P, 2, 2, G, 4, TOK], F16)
        v_sb = sb("v_sb", [P, 2, NU, H, 2, D + 1])
        neg_max = sb("neg_max", [P, 2, NU, H])
        maxt_sb = sb("maxt_sb", [NU * H, P], BF16)
        max_rows = sb("max_rows", [P, 2, NU * H, 64], BF16)
        prob = sb("prob", [P, 2, 1024])
        recip = sb("recip", [P, 8, 2])
        o_sb = sb("o_sb", [P, 2, 2, 8, D])
        ctxt_sb = sb("ctxt_sb", [P, TOK])
        res = sb("res", [P, TT, P])
        stats = sb("stats", [P, TT, 6])
        mean_var = sb("mean_var", [P, TT, 2])
        ve = sb("ve", [P, TT])
        rstd = sb("rstd", [P, TT])
        x1_sb = sb("x1_sb", [P, 2, TT, P])

        consts_in = sem("consts_in")
        bias_in = sem("bias_in")
        made = sem("made")
        constants = sem("constants")
        bqs_ready = sem("bqs_ready")
        dve_made = sem("dve_made")
        x_in = sem("x_in")
        xt_ps = sem("xt_ps")
        xt_ready = sem("xt_ready")
        qk_ps, qk_copied = sem("qk_ps"), sem("qk_copied")
        v_ps, v_copied = sem("v_ps"), sem("v_copied")
        halves = sem("halves")
        xb_ready = sem("xb_ready")
        scratched = sem("scratched")
        s_stacked = sem("s_stacked")
        t_stacked = sem("t_stacked")
        cleared = sem("cleared")
        rows_cleared = sem("rows_cleared")
        s_ready, max_done = sem("s_ready"), sem("max_done")
        maxt_ps, maxt_ready, rows_in = sem("maxt_ps"), sem("maxt_ready"), sem("rows_in")
        st_ready, exp_done, pv_done = sem("st_ready"), sem("exp_done"), sem("pv_done")
        recip_done, norm_done = sem("recip_done"), sem("norm_done")
        ctx_done, ctxt_ready, wo_ps = sem("ctx_done"), sem("ctxt_ready"), sem("wo_ps")
        res_done, stats_done, mv_done = sem("res_done"), sem("stats_done"), sem("mv_done")
        ve_done, rstd_done, x1_done, x1_out = sem("ve_done"), sem("rstd_done"), sem("x1_done"), sem("x1_out")

        w_in, lane_made, euler_made = sem("w_in"), sem("lane_made"), sem("euler_made")
        w_high, w_low = sem("w_high"), sem("w_low")
        xin_in, xt2_ps, xt2_ready = sem("xin_in"), sem("xt2_ps"), sem("xt2_ready")
        x_split = sem("x_split")
        logit_ps, chain = sem("logit_ps"), sem("chain")
        neg_done, expo_done = sem("neg_done"), sem("expo_done")
        gate_ps, up_ps, silu_done, h_done = sem("gate_ps"), sem("up_ps"), sem("silu_done"), sem("h_done")
        y_ps, acc_done = sem("y_ps"), sem("acc_done")
        stats2_done, mv2_done, ve2_done, rstd2_done, y_done, y_out = (
            sem(n) for n in ("stats2_done", "mv2_done", "ve2_done", "rstd2_done", "y_done", "y_out"))

        N_CONST = 8
        LINKS = 11

        def after(eng, semaphore, count):
            if not isinstance(count, int) or count > 0:
                eng.wait_ge(semaphore, count)

        def settle(eng):
            eng.nop(nofuse=True)

        def there(k):
            return not isinstance(k, int) or k < STEPS

        def all_steps(eng, step):
            step(0, 0, True, False)
            step(1, 1, False, False)
            with eng.Fori(1, STEPS // 2 - 2) as t:
                step(2 * t, 0, False, False)
                step(2 * t + 1, 1, False, False)
            for i in range(STEPS - 4, STEPS):
                step(i, i % 2, False, i == STEPS - 1)

        with nc.Block() as block:
            @block.sync
            def _(sp):
                for dst, src in ((w_q, wq), (w_k, wk), (w_v, wv), (w_o, wo)):
                    sp.dma_start(dst[:, :], src).then_inc(consts_in, 16)
                for dst, src in ((b_q, bq), (b_k, bk), (b_v, bv)):
                    sp.dma_start(dst[:, :], src.rearrange("(p a) -> p a", a=1)).then_inc(consts_in, 16)
                sp.dma_start(b_o[:, :], bo.rearrange("(a d) -> a d", a=1).to_broadcast([P, DM])).then_inc(consts_in, 16)

                def load(k, par):
                    after(sp, xt_ps, k)
                    settle(sp)
                    after(sp, xb_ready, k - 1)
                    settle(sp)
                    sp.dma_start(x_sb[:, par, :, :], x_steps[k]).then_inc(x_in, 16)

                load(0, 0)
                for n, src in ((0, bias), (1, bias_t)):
                    for rows in (0, 64):
                        sp.dma_start(prob[rows:rows + 64, n, :], src).then_inc(bias_in, 16)

                def halves_out(k, par):
                    after(sp, s_stacked, 80 * (k - 1))
                    settle(sp)
                    after(sp, t_stacked, 80 * (k - 1))
                    settle(sp)
                    for n in range(2):
                        sp.wait_ge(halves, 4 * k + 2 * n + 2)
                        settle(sp)
                        for c in range(C):
                            part = c % 2 if n == 0 else c // 2
                            sp.dma_start(scratch[par, n, :, c, :, :], qk_hl[:, n, part, :]).then_inc(scratched, 16)
                    sp.wait_ge(scratched, 16 * 2 * C * (k + 1))
                    settle(sp)

                def stacks(k, par, n, signal):
                    after(sp, signal, 80 * k)
                    settle(sp)
                    if isinstance(k, int) and k < 2:
                        sp.wait_ge(cleared, k + 1)
                        settle(sp)
                    sp.dma_start(stack[:, par, n, :, :],
                                 scratch[par, n].rearrange("j c (d g) t -> (j c d) g t", g=G)).then_inc(signal, 16)
                    for j in range(4):
                        sp.dma_start(blocks[32 * j:32 * j + 32, par, 1 - n, :, j, :],
                                     scratch[par, 1 - n, j].rearrange("c (d g) t -> (c d) g t", g=G)).then_inc(signal, 16)

                def stacks_s(k, par):
                    after(sp, s_ready, NU * (k - 1))
                    settle(sp)
                    stacks(k, par, 0, s_stacked)

                def stacks_t(k, par):
                    after(sp, st_ready, NU * (k - 1))
                    settle(sp)
                    stacks(k, par, 1, t_stacked)

                def weights():
                    sp.dma_start(rw_sb[:, :], rw_t).then_inc(w_in, 16)
                    sp.dma_start(wgu_sb[:, :, 0:HID], wg.rearrange("e d h -> d e h")).then_inc(w_in, 16)
                    sp.dma_start(wgu_sb[:, :, HID:2 * HID], wu.rearrange("e d h -> d e h")).then_inc(w_in, 16)
                    sp.dma_start(wd_sb[:, :, :, :], wd.rearrange("e (n p) d -> p e n d", p=P)).then_inc(w_in, 16)

                def rows(k, par):
                    after(sp, st_ready, NU * (k - 1))
                    settle(sp)
                    sp.wait_ge(maxt_ready, k + 1)
                    settle(sp)
                    for a in range(2):
                        sp.dma_start(max_rows[a:a + 1, par, :, :], maxt_sb[:, 64 * a:64 * a + 64]).then_inc(rows_in, 16)

                def store(k, par):
                    sp.wait_ge(x1_done, k + 1)
                    settle(sp)
                    sp.dma_start(x1_steps[k], x1_sb[:, par, :, :]).then_inc(x1_out, 16)

                def step(i, par, first, last):
                    if there(i + 1):
                        stacks_t(i + 1, 1 - par)
                    if there(i + 3):
                        load(i + 3, 1 - par)
                    if not first:
                        store(i - 1, 1 - par)
                    if there(i + 2):
                        halves_out(i + 2, par)
                        stacks_s(i + 2, par)
                    if there(i + 1):
                        rows(i + 1, 1 - par)

                load(1, 1)
                halves_out(0, 0)
                stacks_s(0, 0)
                stacks_t(0, 0)
                load(2, 0)
                halves_out(1, 1)
                stacks_s(1, 1)
                sp.wait_ge(rows_cleared, 1)
                rows(0, 0)
                weights()
                all_steps(sp, step)
                store(STEPS - 1, 1)
                sp.wait_ge(x1_out, 16 * STEPS)

            @block.gpsimd
            def _(pool):
                count = [0]

                def link(ins):
                    count[0] += 1
                    ins.then_inc(made, 1)
                    pool.wait_ge(made, count[0])

                link(pool.memset(ident[:, :], 0.0))
                link(pool.affine_select(out=ident[:, :], in_=ident[:, :], compare_op=ALU.not_equal, fill=1.0, base=0,
                                        pattern=[[-1, P]], channel_multiplier=1))
                link(pool.memset(fold_f[:, :], 0.0))
                for base in (0, 64, -64):
                    link(pool.affine_select(out=fold_f[:, :], in_=fold_f[:, :], compare_op=ALU.not_equal, fill=1.0,
                                            base=base, pattern=[[-1, P]], channel_multiplier=1))
                link(pool.tensor_copy(fold[:, :], fold_f[:, :]))
                link(pool.memset(half[:, :], 1.0))
                link(pool.affine_select(out=half[:, :], in_=half[:, :], compare_op=ALU.is_ge, fill=0.0, base=0,
                                        pattern=[[1, P]], channel_multiplier=-64))
                link(pool.affine_select(out=half[:, :], in_=half[:, :], compare_op=ALU.is_ge, fill=0.0, base=63,
                                        pattern=[[-1, P]], channel_multiplier=64))
                for n, shares in enumerate(SHARES):
                    for q in range(4):
                        link(pool.tensor_scalar(diag[32 * q:32 * q + 32, n, :], fold_f[32 * q:32 * q + 32, 0:64],
                                                shares[q % 2], None, ALU.mult))
                link(pool.memset(v_sb[:, :, :, :, :, :], 0.0))
                for a in range(2):
                    for par in range(2):
                        link(pool.memset(v_sb[64 * a:64 * a + 64, par, :, :, a, D:D + 1], 1.0))
                pool.memset(minus_half[:, :], -0.5).then_inc(constants, 1)

                def add_bias(k, par):
                    pool.wait_ge(x_in, 16 * (k + 1))
                    after(pool, res_done, k - 1)
                    settle(pool)
                    pool.tensor_tensor(xb_sb[:, par, :, :], x_sb[:, par, :, :],
                                       b_o[:, :].unsqueeze(1).to_broadcast([P, TT, P]), ALU.add).then_inc(xb_ready, 1)

                def split(k):
                    after(pool, scratched, 16 * 2 * C * k)
                    for n in range(2):
                        pool.wait_ge(qk_copied, 2 * k + n + 1)
                        settle(pool)
                        pool.tensor_copy(qk_hl[:, n, 0, :], qk_f[:, n, :]).then_inc(halves, 1)
                        pool.wait_ge(halves, 4 * k + 2 * n + 1)
                        pool.tensor_tensor(qk_hl[:, n, 1, :], qk_f[:, n, :], qk_hl[:, n, 0, :], ALU.subtract).then_inc(halves, 1)

                def norm(k, par):
                    pool.wait_ge(mv_done, k + 1)
                    settle(pool)
                    pool.tensor_scalar(ve[:, :], mean_var[:, :, 1], EPS, None, ALU.add).then_inc(ve_done, 1)
                    pool.wait_ge(ve_done, k + 1)
                    pool.tensor_tensor(rstd[:, :], ve[:, :], minus_half[:, :], ALU.pow).then_inc(rstd_done, 1)
                    pool.wait_ge(rstd_done, k + 1)
                    after(pool, x1_out, 16 * k)
                    settle(pool)
                    for t in range(TT):
                        last = pool.tensor_scalar(x1_sb[:, par, t, :], res[:, t, :], mean_var[:, t, 0:1], rstd[:, t:t + 1],
                                                  ALU.subtract, ALU.mult)
                    last.then_inc(x1_done, 1)

                def step(i, par, first, last):
                    if not first:
                        norm(i - 1, 1 - par)
                    if there(i + 1):
                        add_bias(i + 1, 1 - par)
                    if there(i + 2):
                        split(i + 2)

                pool.wait_ge(constants, 1)
                pool.wait_ge(consts_in, 16 * N_CONST)
                split(0)
                add_bias(0, 0)
                split(1)
                all_steps(pool, step)
                norm(STEPS - 1, 1)

            @block.scalar
            def _(act):
                act.wait_ge(consts_in, 16 * N_CONST)
                act.mul(b_qs[:, :], b_q[:, :], SCALE).then_inc(bqs_ready, 1)
                act.wait_ge(bqs_ready, 1)
                act.wait_ge(constants, 1)

                def xt_copy(k, par):
                    act.wait_ge(xt_ps, k + 1)
                    after(act, v_ps, 2 * (k - 1))
                    act.copy(xt_sb[:, par, :], bank[1][:, :]).then_inc(xt_ready, 1)

                def qk_copy(k):
                    for n, (b, s) in enumerate(((b_qs, SCALE), (b_k, 1.0))):
                        act.wait_ge(qk_ps, 2 * k + n + 1)
                        after(act, halves, 4 * k - 2 + 2 * n)
                        act.activation(qk_f[:, n, :], bank[n][:, :], ACT.Identity, bias=b[:, :], scale=s).then_inc(qk_copied, 1)

                def v_copy(k, par, n):
                    u0, u1 = ((0, 4), (4, NU))[n]
                    act.wait_ge(v_ps, 2 * k + n + 1)
                    after(act, pv_done, NU * (k - 1))
                    for a in range(2):
                        rows = slice(64 * a, 64 * a + 64)
                        last = act.copy(v_sb[rows, par, u0:u1, :, a, 0:D],
                                        bank[n][rows, 0:(u1 - u0) * P].rearrange("p (u h d) -> p u h d", h=H, d=D))
                    last.then_inc(v_copied, 1)

                def ctx_copy(k):
                    act.wait_ge(ctx_done, NU * (k + 1))
                    after(act, wo_ps, k)
                    act.activation(ctxt_sb[:, :], ctx_ps[:, :], ACT.Identity, bias=b_v[:, :], scale=1.0).then_inc(ctxt_ready, 1)

                def step(i, par, first, last):
                    if not first:
                        ctx_copy(i - 1)
                    for u in range(NU):
                        act.wait_ge(st_ready, NU * i + u + 1)
                        after(act, pv_done, NU * i + u - 1)
                        act.activation(prob[:, (par + u) % 2, :], scoret_ps[:, :, :].rearrange("p b c -> p (b c)"),
                                       ACT.Exp).then_inc(exp_done, 1)
                        if u == 0 and there(i + 2):
                            xt_copy(i + 2, par)
                        if u == 1 and there(i + 2):
                            qk_copy(i + 2)
                        if u == 2 and there(i + 1):
                            v_copy(i + 1, 1 - par, 0)
                    if there(i + 1):
                        v_copy(i + 1, 1 - par, 1)

                for k in range(2):
                    xt_copy(k, k)
                    qk_copy(k)
                v_copy(0, 0, 0)
                v_copy(0, 0, 1)
                all_steps(act, step)
                ctx_copy(STEPS - 1)

            @block.vector
            def _(dve):
                dve.memset(blocks[:, 0, :, :, :, :], 0.0).then_inc(cleared, 1)
                dve.wait_ge(bias_in, 64)
                dve.tensor_copy(bias_hl[:, :, :], prob[:, :, :]).then_inc(dve_made, 1)
                dve.wait_ge(dve_made, 1)
                dve.tensor_tensor(bias_hl[64:128, :, :], prob[64:128, :, :], bias_hl[64:128, :, :],
                                  ALU.subtract).then_inc(dve_made, 1)
                dve.memset(max_rows[:, :, :, :], 0.0).then_inc(rows_cleared, 1)
                dve.memset(blocks[:, 1, :, :, :, :], 0.0).then_inc(cleared, 1)

                def maximum(k, par, v):
                    dve.wait_ge(s_ready, NU * k + v + 1)
                    dve.tensor_reduce(neg_max[:, par, v, :], score_ps[:, :, :].rearrange("p b (h k) -> p (b h) k", k=W),
                                      AX_X, ALU.max, negate=True).then_inc(max_done, 1)

                def max_copy(k):
                    dve.wait_ge(maxt_ps, k + 1)
                    after(dve, rows_in, 32 * k)
                    dve.tensor_copy(maxt_sb[:, :], bank[0][0:NU * H, 0:P]).then_inc(maxt_ready, 1)

                def normalise(i, par, u):
                    n = NU * i + u
                    dve.wait_ge(pv_done, n + 1)
                    o = o_ps[:, 0:288].rearrange("p (h e a d) -> p h e a d", h=8, e=2, a=2)
                    for e in range(2):
                        rows = slice(64 * e, 64 * e + 64)
                        dve.reciprocal(recip[rows, :, :], o[rows, :, e, :, D]).then_inc(recip_done, 1)
                    dve.wait_ge(recip_done, 2 * n + 2)
                    after(dve, ctx_done, n - 1)
                    for e in range(2):
                        rows = slice(64 * e, 64 * e + 64)
                        last = dve.tensor_tensor(o_sb[rows, (par + u) % 2, :, :, :].rearrange("p a h d -> p h a d"),
                                                 o[rows, :, e, :, 0:D],
                                                 recip[rows, :, :].unsqueeze(3).to_broadcast([64, 8, 2, D]), ALU.mult)
                    last.then_inc(norm_done, 1)

                def residual(k, par):
                    dve.wait_ge(wo_ps, k + 1)
                    dve.wait_ge(xb_ready, k + 1)
                    after(dve, x1_done, k)
                    dve.tensor_tensor(res[:, :, :], bank[0][:, :].rearrange("p (t d) -> p t d", t=TT), xb_sb[:, par, :, :],
                                      ALU.add).then_inc(res_done, 1)
                    dve.wait_ge(res_done, k + 1)
                    for t in range(TT):
                        last = dve.bn_stats(stats[:, t, :], res[:, t, :])
                    last.then_inc(stats_done, 1)
                    dve.wait_ge(stats_done, k + 1)
                    settle(dve)
                    for t in range(TT):
                        last = dve.bn_aggr(mean_var[:, t, :], stats[:, t, :])
                    last.then_inc(mv_done, 1)

                def step(i, par, first, last):
                    for u in range(TURNS):
                        if there(i + 1):
                            if u < NU:
                                maximum(i + 1, 1 - par, u)
                            if u == NU:
                                max_copy(i + 1)
                        if u == 0 and not first:
                            residual(i - 1, 1 - par)
                        if 1 <= u <= NU:
                            normalise(i, par, u - 1)

                for v in range(NU):
                    maximum(0, 0, v)
                max_copy(0)
                all_steps(dve, step)
                residual(STEPS - 1, 1)

            @block.tensor
            def _(pe):
                pe.wait_ge(consts_in, 16 * N_CONST)
                pe.wait_ge(constants, 1)

                def turn_x(k, par):
                    pe.wait_ge(x_in, 16 * (k + 1))
                    after(pe, qk_copied, 2 * k)
                    after(pe, v_copied, 2 * (k - 1))
                    for t in range(TT):
                        last = pe.transpose(bank[1][:, t * P:(t + 1) * P], x_sb[:, par, t, :], ident[:, :])
                    last.then_inc(xt_ps, 1)

                def project_qk(k, par):
                    after(pe, maxt_ready, k - 1)
                    after(pe, res_done, k - 2)
                    pe.wait_ge(xt_ready, k + 1)
                    for n, w in enumerate((w_q, w_k)):
                        pe.matmul(bank[n][:, :], w[:, :], xt_sb[:, par, :], start=True, stop=True).then_inc(qk_ps, 1)

                def project_v(k, par, n):
                    if isinstance(k, int) and k == STEPS - 1:
                        if n == 0:
                            pe.wait_ge(res_done, k - 1)
                        else:
                            pe.wait_ge(v_copied, 2 * k)
                    else:
                        pe.wait_ge(qk_copied, 2 * (k + 1) + n + 1)
                    u0, u1 = ((0, 4), (4, NU))[n]
                    for u in range(u0, u1):
                        a, b = UNITS[u]
                        cols = slice((u - u0) * P, (u - u0 + 1) * P)
                        if b == a + W:
                            last = pe.matmul(bank[n][:, cols], xt_sb[:, par, a:a + P], w_v[:, :], start=True, stop=True)
                        else:
                            for r, t0 in ((0, a), (W, b)):
                                last = pe.matmul(bank[n][r:r + W, cols], xt_sb[:, par, t0:t0 + W], w_v[:, :],
                                                 start=True, stop=True)
                    last.then_inc(v_ps, 1)

                def products(ps, par, u, a_of, b_of):
                    for g in range(G):
                        for a in range(2):
                            t0 = UNITS[u][a]
                            last = pe.matmul(ps[64 * a:64 * a + 64, g // 2, (g % 2) * 4 * W:(g % 2 + 1) * 4 * W],
                                             stack[:, par, a_of, g, t0:t0 + W],
                                             blocks[:, par, b_of, g, :, t0:t0 + W],
                                             start=False, stop=True, skip_group_check=True)
                    return last

                def scores(k, par, v):
                    if v == 0:
                        pe.wait_ge(s_stacked, 80 * (k + 1))
                    after(pe, max_done, NU * k + v)
                    for n in range(2):
                        pe.matmul(score_ps[:, n, :], fold[:, :], bias_hl[:, 0, n * 512:n * 512 + 512],
                                  start=True, stop=False, skip_group_check=True)
                    products(score_ps, par, v, 0, 1).then_inc(s_ready, 1)

                def scores_t(i, par, u):
                    if u == 0:
                        pe.wait_ge(t_stacked, 80 * (i + 1))
                        pe.wait_ge(rows_in, 32 * (i + 1))
                    after(pe, exp_done, NU * i + u)
                    for n in range(2):
                        pe.matmul(scoret_ps[:, n, :], fold[:, :], bias_hl[:, 1, n * 512:n * 512 + 512],
                                  start=True, stop=False, skip_group_check=True)
                    for n in range(2):
                        pe.matmul(scoret_ps[:, n, :], half[:, :],
                                  max_rows[:, par, u * H + 8 * n:u * H + 8 * n + 8, :].rearrange("a h q -> a (h q)"),
                                  start=False, stop=False, skip_group_check=True)
                    products(scoret_ps, par, u, 1, 0).then_inc(st_ready, 1)

                def values(i, par, u):
                    n = NU * i + u
                    pe.wait_ge(exp_done, n + 1)
                    if u == 0:
                        pe.wait_ge(v_copied, 2 * (i + 1))
                    after(pe, norm_done, n)
                    for h in range(8):
                        last = pe.matmul(o_ps[:, h * 36:h * 36 + 36], prob[:, (par + u) % 2, h * P:(h + 1) * P],
                                         v_sb[:, par, u, 2 * h:2 * h + 2, :, :].rearrange("p h a d -> p (h a d)"),
                                         start=True, stop=True)
                    last.then_inc(pv_done, 1)

                def context(i, par, u):
                    pe.wait_ge(norm_done, NU * i + u + 1)
                    if u == 0:
                        after(pe, ctxt_ready, i)
                    settle(pe)
                    for a in range(2):
                        t0 = UNITS[u][a]
                        for e in range(2):
                            rows = slice(64 * e, 64 * e + 64)
                            last = pe.matmul(ctx_ps[rows, t0:t0 + W],
                                             o_sb[rows, (par + u) % 2, a, :, :].rearrange("p h d -> p (h d)"),
                                             diag[rows, share(t0), :], start=(u == 0 and a == 0), stop=(u == NU - 1),
                                             skip_group_check=True)
                    last.then_inc(ctx_done, 1)

                def project_out(k):
                    pe.wait_ge(ctxt_ready, k + 1)
                    if there(k + 1):
                        pe.wait_ge(maxt_ready, k + 2)
                    for t in range(TT):
                        last = pe.matmul(bank[0][:, t * P:(t + 1) * P], ctxt_sb[:, t * P:(t + 1) * P], w_o[:, :],
                                         start=True, stop=True)
                    last.then_inc(wo_ps, 1)

                def turn_maxima(k, par):
                    pe.wait_ge(max_done, NU * (k + 1))
                    pe.wait_ge(v_copied, 2 * k + 1)
                    pe.transpose(bank[0][0:NU * H, 0:P], neg_max[:, par, :, :].rearrange("p u h -> p (u h)"),
                                 ident[:, :]).then_inc(maxt_ps, 1)

                def step(i, par, first, last):
                    for u in range(TURNS):
                        if u < NU:
                            scores_t(i, par, u)
                            if there(i + 1):
                                scores(i + 1, 1 - par, u)
                        if u == 0:
                            if not first:
                                project_out(i - 1)
                            if there(i + 2):
                                turn_x(i + 2, par)
                        if u == NU and there(i + 1):
                            turn_maxima(i + 1, 1 - par)
                        if u == NU + 1 and there(i + 1):
                            project_v(i + 1, 1 - par, 1)
                        if u >= 2:
                            context(i, par, u - 2)
                        if 1 <= u <= NU:
                            values(i, par, u - 1)
                        if u == 1 and there(i + 2):
                            project_qk(i + 2, par)
                        if u == 2 and there(i + 1):
                            project_v(i + 1, 1 - par, 0)

                for k in range(2):
                    turn_x(k, k)
                    project_qk(k, k)
                project_v(0, 0, 0)
                project_v(0, 0, 1)
                pe.wait_ge(dve_made, 2)
                for v in range(NU):
                    scores(0, 0, v)
                turn_maxima(0, 0)
                all_steps(pe, step)
                project_out(STEPS - 1)

        attention.close()

        def sb(name, shape, dt=F32):
            return ctx.enter_context(nc.sbuf_tensor(name, shape, dt))

        wgu_hi = sb("wgu_hi", [P, E, 2 * HID], F32R)
        wgu_lo = sb("wgu_lo", [P, E, 2 * HID], F32R)
        lane = sb("lane", [P, E])
        euler = sb("euler", [P, 2 * TT])
        xin = sb("xin", [P, 2, TT, P])
        xt2 = sb("xt2", [P, 2, TOK])
        x_hi, x_lo = sb("x_hi", [P, 2, TOK], F32R), sb("x_lo", [P, 2, TOK], F32R)
        logit, top = sb("logit", [P, TT, E]), sb("top", [P, TT, E])
        top_at = sb("top_at", [P, TT, E], U32)
        top_f = sb("top_f", [P, TT, 2])
        neg_top, expo, expo1 = (sb(n, [P, 2 * TT]) for n in ("neg_top", "expo", "expo1"))
        gate2, gnorm = sb("gate2", [P, TT, 2]), sb("gnorm", [P, TT, 2])
        gsum, ginv = sb("gsum", [P, TT]), sb("ginv", [P, TT])
        pick, picked = sb("pick", [P, 2, TT, E]), sb("picked", [P, 2, TT, E])
        share_e = sb("share_e", [P, 2, TT, E])
        silu_sb = sb("silu_sb", [P, 2, TOK])
        h_sb = sb("h_sb", [P, 2, 2, TOK])
        acc = sb("acc", [P, 2, TT, P])
        stats2, mv2 = sb("stats2", [P, TT, 6]), sb("mv2", [P, TT, 2])
        ve2, rstd2 = sb("ve2", [P, TT]), sb("rstd2", [P, TT])
        y_sb = sb("y_sb", [P, 2, TT, P])

        with nc.Block() as block:
            def all_chunks(eng, chunk):
                chunk(0, 0, True, False)
                chunk(1, 1, False, False)
                with eng.Fori(1, CHUNKS // 2 - 1) as t:
                    chunk(2 * t, 0, False, False)
                    chunk(2 * t + 1, 1, False, False)
                chunk(CHUNKS - 2, 0, False, False)
                chunk(CHUNKS - 1, 1, False, True)

            @block.sync
            def _(sp):
                def load(k, par):
                    after(sp, xt2_ps, k)
                    after(sp, acc_done, E * (k - 2) + 1)
                    settle(sp)
                    sp.dma_start(xin[:, par, :, :], x1_steps[k]).then_inc(xin_in, 16)

                def store(k, par):
                    sp.wait_ge(y_done, k + 1)
                    settle(sp)
                    sp.dma_start(out_steps[k], y_sb[:, par, :, :]).then_inc(y_out, 16)

                def chunk(i, par, first, last):
                    if not last:
                        load(i + 1, 1 - par)
                    if not first:
                        store(i - 1, 1 - par)

                load(0, 0)
                all_chunks(sp, chunk)
                store(CHUNKS - 1, 1)
                sp.wait_ge(y_out, 16 * CHUNKS)

            @block.gpsimd
            def _(pool):
                pool.memset(euler[:, :], EULER).then_inc(euler_made, 1)
                pool.iota(lane[:, :], pattern=[[1, E]], base=0, channel_multiplier=0,
                          allow_small_or_imprecise_dtypes=True).then_inc(lane_made, 1)
                pool.wait_ge(euler_made, 1)

                def powers(k):
                    pool.wait_ge(neg_done, k + 1)
                    settle(pool)
                    pool.tensor_tensor(expo[:, :], euler[:, :], neg_top[:, :], ALU.pow).then_inc(expo_done, 1)

                def norm(k, par):
                    pool.wait_ge(mv2_done, k + 1)
                    settle(pool)
                    pool.tensor_scalar(ve2[:, :], mv2[:, :, 1], EPS, None, ALU.add).then_inc(ve2_done, 1)
                    pool.wait_ge(ve2_done, k + 1)
                    pool.tensor_tensor(rstd2[:, :], ve2[:, :], minus_half[:, :], ALU.pow).then_inc(rstd2_done, 1)
                    pool.wait_ge(rstd2_done, k + 1)
                    after(pool, y_out, 16 * k)
                    settle(pool)
                    for t in range(TT):
                        last = pool.tensor_scalar(y_sb[:, par, t, :], acc[:, par, t, :], mv2[:, t, 0:1],
                                                  rstd2[:, t:t + 1], ALU.subtract, ALU.mult)
                    last.then_inc(y_done, 1)

                def chunk(i, par, first, last):
                    if not first:
                        norm(i - 1, 1 - par)
                    if not last:
                        powers(i + 1)

                powers(0)
                all_chunks(pool, chunk)
                norm(CHUNKS - 1, 1)

            @block.scalar
            def _(act):
                def turned(k, par):
                    act.wait_ge(xt2_ps, k + 1)
                    after(act, logit_ps, k - 1)
                    after(act, x_split, 2 * (k - 1))
                    settle(act)
                    act.copy(xt2[:, par, :], bank[0][:, :]).then_inc(xt2_ready, 1)

                def silu(m, hh):
                    act.wait_ge(gate_ps, 2 * m + hh + 1)
                    after(act, h_done, 2 * m + hh - 1)
                    act.activation(silu_sb[:, hh, :], (score_ps, scoret_ps)[hh][:, 0, :], ACT.Silu).then_inc(silu_done, 1)

                def chunk(i, par, first, last):
                    for e in range(E):
                        for hh in range(2):
                            silu(E * i + e, hh)
                        if e == 2 and not last:
                            turned(i + 1, 1 - par)

                act.wait_ge(w_in, 64)
                turned(0, 0)
                for e in range(E):
                    act.copy(wgu_hi[:, e, :], wgu_sb[:, e, :]).then_inc(w_high, 1)
                all_chunks(act, chunk)

            @block.vector
            def _(dve):


                def link(ins, k, n):
                    ins.then_inc(chain, 1)
                    dve.wait_ge(chain, LINKS * k + n)
                    settle(dve)

                def split(k, par):
                    dve.wait_ge(xt2_ready, k + 1)
                    after(dve, up_ps, 2 * E * (k - 1))
                    settle(dve)
                    dve.tensor_copy(x_hi[:, par, :], xt2[:, par, :]).then_inc(x_split, 1)
                    dve.wait_ge(x_split, 2 * k + 1)
                    dve.tensor_tensor(x_lo[:, par, :], xt2[:, par, :], x_hi[:, par, :].bitcast(F32),
                                      ALU.subtract).then_inc(x_split, 1)

                def top_two(k):
                    dve.wait_ge(logit_ps, k + 1)
                    settle(dve)
                    link(dve.tensor_copy(logit[:, :, :], bank[1][:, 0:TT * E].rearrange("p (t e) -> p t e", t=TT)), k, 1)
                    for t in range(TT):
                        last = dve.max(top[:, t, :], logit[:, t, :])
                    link(last, k, 2)
                    dve.tensor_scalar(neg_top[:, :].rearrange("p (t c) -> p t c", t=TT), top[:, :, 0:2], -1.0, None,
                                      ALU.mult).then_inc(neg_done, 1)
                    for t in range(TT):
                        last = dve.max_index(top_at[:, t, :], top[:, t, :], logit[:, t, :])
                    link(last, k, 3)
                    link(dve.tensor_copy(top_f[:, :, :], top_at[:, :, 0:2]), k, 4)

                def shares(k, par):
                    dve.wait_ge(expo_done, k + 1)
                    settle(dve)
                    link(dve.tensor_scalar(expo1[:, :], expo[:, :], 1.0, None, ALU.add), k, 5)
                    link(dve.reciprocal(gate2[:, :, :].rearrange("p t c -> p (t c)"), expo1[:, :]), k, 6)
                    link(dve.scalar_tensor_tensor(out=gsum[:, :], in0=gate2[:, :, 0], scalar=1e-10, in1=gate2[:, :, 1],
                                                  op0=ALU.add, op1=ALU.add), k, 7)
                    link(dve.reciprocal(ginv[:, :], gsum[:, :]), k, 8)
                    dve.tensor_tensor(gnorm[:, :, :], gate2[:, :, :],
                                      ginv[:, :].unsqueeze(2).to_broadcast([P, TT, 2]), ALU.mult)
                    for c in range(2):
                        last = dve.tensor_tensor(pick[:, c, :, :], lane[:, :].unsqueeze(1).to_broadcast([P, TT, E]),
                                                 top_f[:, :, c:c + 1].to_broadcast([P, TT, E]), ALU.is_equal)
                    link(last, k, 9)
                    for c in range(2):
                        last = dve.tensor_tensor(picked[:, c, :, :], pick[:, c, :, :],
                                                 gnorm[:, :, c:c + 1].to_broadcast([P, TT, E]), ALU.mult)
                    link(last, k, 10)
                    link(dve.tensor_tensor(share_e[:, par, :, :], picked[:, 0, :, :], picked[:, 1, :, :], ALU.add), k, 11)

                def hidden(m, b, hh):
                    dve.wait_ge(silu_done, 2 * m + hh + 1)
                    dve.wait_ge(up_ps, 2 * m + hh + 1)
                    after(dve, y_ps, m - 1)
                    dve.tensor_tensor(h_sb[:, b, hh, :], silu_sb[:, hh, :], (score_ps, scoret_ps)[hh][:, 1, :],
                                      ALU.mult).then_inc(h_done, 1)

                def add(i, par, e):
                    m = E * i + e
                    dve.wait_ge(y_ps, m + 1)
                    after(dve, acc_done, m)
                    if e == 0:
                        after(dve, y_done, i - 1)
                        settle(dve)
                    y = (o_ps, ctx_ps)[e % 2]
                    for t in range(TT):
                        cols = slice(t * P, (t + 1) * P)
                        last = dve.scalar_tensor_tensor(out=acc[:, par, t, :], in0=y[:, cols],
                                                        scalar=share_e[:, par, t, e:e + 1],
                                                        in1=acc[:, par, t, :] if e else xin[:, par, t, :],
                                                        op0=ALU.mult, op1=ALU.add)
                    last.then_inc(acc_done, 1)

                def statistics(k, par):
                    dve.wait_ge(acc_done, E * (k + 1))
                    after(dve, y_done, k)
                    settle(dve)
                    for t in range(TT):
                        last = dve.bn_stats(stats2[:, t, :], acc[:, par, t, :])
                    last.then_inc(stats2_done, 1)
                    dve.wait_ge(stats2_done, k + 1)
                    settle(dve)
                    for t in range(TT):
                        last = dve.bn_aggr(mv2[:, t, :], stats2[:, t, :])
                    last.then_inc(mv2_done, 1)

                def chunk(i, par, first, last):
                    for e in range(E):
                        for hh in range(2):
                            hidden(E * i + e, e % 2, hh)
                        if e:
                            add(i, par, e - 1)
                        elif not first:
                            add(i - 1, 1 - par, E - 1)
                        if e == 1 and not first:
                            statistics(i - 1, 1 - par)
                        if not last:
                            if e == 3:
                                split(i + 1, 1 - par)
                            if e == 5:
                                top_two(i + 1)
                            if e == 6:
                                shares(i + 1, 1 - par)

                dve.wait_ge(lane_made, 1)
                split(0, 0)
                for e in range(E):
                    dve.wait_ge(w_high, e + 1)
                    dve.tensor_tensor(wgu_lo[:, e, :], wgu_sb[:, e, :], wgu_hi[:, e, :].bitcast(F32),
                                      ALU.subtract).then_inc(w_low, 1)
                top_two(0)
                shares(0, 0)
                all_chunks(dve, chunk)
                add(CHUNKS - 1, 1, E - 1)
                statistics(CHUNKS - 1, 1)

            @block.tensor
            def _(pe):
                pe.wait_ge(w_in, 64)

                def turn(k, par):
                    pe.wait_ge(xin_in, 16 * (k + 1))
                    after(pe, xt2_ready, k)
                    for t in range(TT):
                        last = pe.transpose(bank[0][:, t * P:(t + 1) * P], xin[:, par, t, :], ident[:, :])
                    last.then_inc(xt2_ps, 1)

                def logits(k, par):
                    pe.wait_ge(xt2_ready, k + 1)
                    after(pe, chain, LINKS * (k - 1) + 1)
                    for t in range(TT):
                        last = pe.matmul(bank[1][:, t * E:(t + 1) * E], xt2[:, par, t * P:(t + 1) * P], rw_sb[:, :],
                                         start=True, stop=True)
                    last.then_inc(logit_ps, 1)

                def gate_up(i, par, e, hh, first):
                    m = E * i + e
                    after(pe, h_done, 2 * m + hh - 1)
                    if first:
                        pe.wait_ge(w_low, e + 1)
                    if e == 0 and hh == 0:
                        pe.wait_ge(x_split, 2 * (i + 1))
                    for n, signal in ((0, gate_ps), (1, up_ps)):
                        cols = slice(n * HID + hh * P, n * HID + hh * P + P)
                        out_ps = (score_ps, scoret_ps)[hh][:, n, :]
                        pe.matmul(out_ps, wgu_hi[:, e, cols], x_lo[:, par, :], start=True, stop=False)
                        pe.matmul(out_ps, wgu_lo[:, e, cols], x_hi[:, par, :], start=False, stop=False)
                        pe.matmul(out_ps, wgu_hi[:, e, cols], x_hi[:, par, :], start=False, stop=True).then_inc(signal, 1)

                def down(m, e):
                    pe.wait_ge(h_done, 2 * m + 2)
                    after(pe, acc_done, m - 1)
                    y = (o_ps, ctx_ps)[e % 2]
                    for t in range(TT):
                        cols = slice(t * P, (t + 1) * P)
                        for c in range(2):
                            last = pe.matmul(y[:, cols], h_sb[:, e % 2, c, cols], wd_sb[:, e, c, :],
                                             start=(c == 0), stop=(c == 1))
                    last.then_inc(y_ps, 1)

                def chunk(i, par, first, last):
                    for e in range(E):
                        for hh in range(2):
                            gate_up(i, par, e, hh, first)
                        if e or not first:
                            down(E * i + e - 1, (e - 1) % E)
                        if not last:
                            if e == 1:
                                turn(i + 1, 1 - par)
                            if e == 3:
                                logits(i + 1, 1 - par)

                turn(0, 0)
                logits(0, 0)
                all_chunks(pe, chunk)
                down(E * CHUNKS - 1, E - 1)



def kernel(**inputs):
    import numpy as np
    import concourse.bacc as bacc
    from concourse import mybir as mb
    from concourse.bass_utils import run_bass_kernel_spmd

    a = {n.replace("L0_attn_", "").replace("L0_ffn_", ""): np.asarray(v) for n, v in inputs.items()}
    qk = np.array([8 * (4 * g + j) + d for j in range(4) for d in range(D) for g in range(G)])
    order = np.empty(H, int)
    for j in range(4):
        for g in range(G):
            order[place(j, g)] = 4 * g + j
    vals = np.array([8 * h + d for h in order for d in range(D)])
    turned = np.array([8 * h + d for h in np.concatenate([order[0::2], order[1::2]]) for d in range(D)])
    bias = a["pos_bias"][order]
    arrays = {
        "x": a["hidden_states"], "wq": a["Wq"][:, qk], "bq": a["bq"][qk], "wk": a["Wk"][:, qk], "bk": a["bk"][qk],
        "wv": a["Wv"][:, vals], "bv": a["bv"][turned], "wo": a["Wo"][turned], "bo": a["bo"],
        "bias": bias.transpose(1, 0, 2).reshape(W, H * W), "bias_t": bias.transpose(2, 0, 1).reshape(W, H * W),
        "rw_t": a["router_w"].T, "wg": a["w_gate"], "wu": a["w_up"], "wd": a["w_down"],
    }
    nc = bacc.Bacc("TRN2", target_bir_lowering=False, num_devices=1)
    feeds, args = {}, []
    for name, v in arrays.items():
        v = np.ascontiguousarray(v)
        feeds[f"in_{name}"] = v
        args.append(nc.dram_tensor(f"in_{name}", v.shape, mb.dt.from_np(v.dtype), kind="ExternalInput").ap())
    args.append(nc.dram_tensor("out_0", (B, S, DM), mb.dt.float32, kind="ExternalOutput").ap())
    build(nc, *args)
    r = run_bass_kernel_spmd(nc, [feeds], core_ids=[0])
    return r.results[0]["out_0"]
```

```python
from contextlib import ExitStack

import concourse.bass as bass
from concourse import mybir

F32 = mybir.dt.float32
F32R = mybir.dt.float32r
F16 = mybir.dt.float16
BF16 = mybir.dt.bfloat16
U32 = mybir.dt.uint32
I32 = mybir.dt.int32
ALU = mybir.AluOpType
ACT = mybir.ActivationFunctionType
AX_X = mybir.AxisListType.X

P = 128
B, S, DM = 32, 256, 128
H, W, STRIDE = 16, 64, 32
D = DM // H
E, HID = 8, 256
EPS = 1e-5
EULER = 2.718281828459045
SCALE = 1.0 / float(D) ** 0.5

STEPS = B // 2
TOK = 2 * S
TT = TOK // P
CHUNKS = B * S // TOK
N_TOK = B * S
TOP = 2
ROW = DM + 2
REGION = N_TOK + TOK
FULL = TOP * N_TOK // TOK
SPARE = E - 1
SLOT_CHUNKS = FULL + SPARE
AHEAD = 4
G = 4
C = 4
UNITS = [(0, 64), (128, 192), (256, 320), (384, 448), (32, 96), (288, 352), (160, 416)]
NU = len(UNITS)
SHARES = [(1.0, 0.5), (0.5, 0.5), (0.5, 1.0 / 3.0), (2.0 / 3.0, 1.0)]
TURNS = NU + 2


def share(first_token):
    w = (first_token % S) // STRIDE
    return 0 if w == 0 else 3 if w == 6 else 2 if w == 5 else 1


def place(j, g):
    return 4 * g + j


def build(nc, x, wq, bq, wk, bk, wv, bv, wo, bo, bias, bias_t, rw_t, wg, wu, wd, out):
    x1_dram = nc.dram_tensor("x1_dram", (B * S, DM), F32, kind="Internal").ap()
    scratch = nc.dram_tensor("scratch", (2, 2, 4, C, D * G, TOK), F16, kind="Internal").ap()
    slots = nc.dram_tensor("slots", (E * REGION + SPARE * TOK, ROW), F32, kind="Internal").ap()
    results = nc.dram_tensor("results", (TOP * N_TOK + (E + SPARE) * TOK, DM), F32, kind="Internal").ap()
    results_steps = results[0:TOP * N_TOK, :].rearrange("(i t p c) d -> i p t c d", t=TT, p=P, c=TOP)
    x_steps = x.rearrange("b s d -> (b s) d").rearrange("(i t p) d -> i p t d", t=TT, p=P)
    x1_steps = x1_dram.rearrange("(i t p) d -> i p t d", t=TT, p=P)
    out_steps = out.rearrange("b s d -> (b s) d").rearrange("(i t p) d -> i p t d", t=TT, p=P)

    with ExitStack() as ctx:
        def sb(name, shape, dt=F32):
            return ctx.enter_context(nc.sbuf_tensor(name, shape, dt))

        def sem(name):
            return ctx.enter_context(nc.semaphore(name))

        bank = [ctx.enter_context(nc.psum_tensor(f"bank{i}", [P, 512], F32)) for i in range(2)]
        score_ps = ctx.enter_context(nc.psum_tensor("score_ps", [P, 2, 512], F32))
        scoret_ps = ctx.enter_context(nc.psum_tensor("scoret_ps", [P, 2, 512], F32))
        o_ps = ctx.enter_context(nc.psum_tensor("o_ps", [P, 512], F32))
        ctx_ps = ctx.enter_context(nc.psum_tensor("ctx_ps", [P, 512], F32))

        ident = sb("ident", [P, P])
        fold_f = sb("fold_f", [P, P])
        fold = sb("fold", [P, P], F16)
        half = sb("half", [P, P], BF16)
        diag = sb("diag", [P, 4, 64])
        minus_half = sb("minus_half", [P, TT])
        w_q, w_k, w_v, w_o = (sb(n, [P, P]) for n in ("w_q", "w_k", "w_v", "w_o"))
        b_q, b_k, b_v, b_qs = (sb(n, [P, 1]) for n in ("b_q", "b_k", "b_v", "b_qs"))
        b_o = sb("b_o", [P, P])
        bias_hl = sb("bias_hl", [P, 2, 1024], F16)

        wgu_sb = sb("wgu_sb", [P, E, 2 * HID])
        wd_sb = sb("wd_sb", [P, E, 2, P])
        rw_sb = sb("rw_sb", [P, E])

        lane = sb("lane", [P, E])
        counts = sb("counts", [P, 2, E])
        fill = sb("fill", [P, E, TT, ROW])

        rows_sb = sb("rows_sb", [P, TOP, TT, ROW])
        slot_at = sb("slot_at", [P, TOP * TT], U32)
        fill_at = sb("fill_at", [P, E], I32)

        attention = ExitStack()

        def sb(name, shape, dt=F32):
            return attention.enter_context(nc.sbuf_tensor(name, shape, dt))

        x_sb = sb("x_sb", [P, 2, TT, P])
        xb_sb = sb("xb_sb", [P, 2, TT, P])
        xt_sb = sb("xt_sb", [P, 2, TOK])
        qk_f = sb("qk_f", [P, 2, TOK])
        qk_hl = sb("qk_hl", [P, 2, 2, TOK], F16)
        stack = sb("stack", [P, 2, 2, G, TOK], F16)
        blocks = sb("blocks", [P, 2, 2, G, 4, TOK], F16)
        v_sb = sb("v_sb", [P, 2, NU, H, 2, D + 1])
        neg_max = sb("neg_max", [P, 2, NU, H])
        maxt_sb = sb("maxt_sb", [NU * H, P], BF16)
        max_rows = sb("max_rows", [P, NU * H, 64], BF16)
        prob = sb("prob", [P, 2, 1024])
        recip = sb("recip", [P, 8, 2])
        o_sb = sb("o_sb", [P, 2, 2, 8, D])
        ctxt_sb = sb("ctxt_sb", [P, TOK])
        res = sb("res", [P, TT, P])
        stats = sb("stats", [P, TT, 6])
        mean_var = sb("mean_var", [P, TT, 2])
        ve = sb("ve", [P, TT])
        rstd = sb("rstd", [P, TT])
        x1_sb = sb("x1_sb", [P, 2, TT, P])

        tri = sb("tri", [P, P], BF16)
        ones = sb("ones", [P, P], BF16)
        euler = sb("euler", [P, TOP * TT])
        x1t_sb = sb("x1t_sb", [P, TOK])
        logit, top = sb("logit", [P, TT, E]), sb("top", [P, TT, E])
        top_at = sb("top_at", [P, TT, E], U32)
        top_f = sb("top_f", [P, TT, TOP])
        neg_top, expo, expo1 = (sb(n, [P, TOP * TT]) for n in ("neg_top", "expo", "expo1"))
        gate2 = sb("gate2", [P, TT, TOP])
        gsum, ginv = sb("gsum", [P, TT]), sb("ginv", [P, TT])
        pick = sb("pick", [P, TOP, TT, E])
        member = sb("member", [P, TT + 1, E], BF16)
        slot_of = sb("slot_of", [P, TT, E])
        picked = sb("picked", [P, TOP, TT, E])
        slot_f = sb("slot_f", [P, TOP * TT])

        x1t_ps, x1t_ready, rows_made = sem("x1t_ps"), sem("x1t_ready"), sem("rows_made")
        logit_ps, chain, neg_done, expo_done = sem("logit_ps"), sem("chain"), sem("neg_done"), sem("expo_done")
        rank_ps, scattered = sem("rank_ps"), sem("scattered")
        consts_in = sem("consts_in")
        bias_in = sem("bias_in")
        made = sem("made")
        first_constants = sem("first_constants")
        constants = sem("constants")
        bqs_ready = sem("bqs_ready")
        dve_made = sem("dve_made")
        x_in = sem("x_in")
        xt_ps = sem("xt_ps")
        xt_ready = sem("xt_ready")
        qk_ps, qk_copied = sem("qk_ps"), sem("qk_copied")
        v_ps, v_copied = sem("v_ps"), sem("v_copied")
        halves = sem("halves")
        xb_ready = sem("xb_ready")
        scratched = sem("scratched")
        s_stacked = sem("s_stacked")
        t_stacked = sem("t_stacked")
        cleared = sem("cleared")
        rows_cleared = sem("rows_cleared")
        s_ready, max_done = sem("s_ready"), sem("max_done")
        maxt_ps, maxt_ready, rows_in = sem("maxt_ps"), sem("maxt_ready"), sem("rows_in")
        st_ready, exp_done, pv_done = sem("st_ready"), sem("exp_done"), sem("pv_done")
        recip_done, norm_done = sem("recip_done"), sem("norm_done")
        ctx_done, ctxt_ready, wo_ps = sem("ctx_done"), sem("ctxt_ready"), sem("wo_ps")
        res_done, stats_done, mv_done = sem("res_done"), sem("stats_done"), sem("mv_done")
        ve_done, rstd_done, x1_done, x1_out = sem("ve_done"), sem("rstd_done"), sem("x1_done"), sem("x1_out")

        w_in, rw_in = sem("w_in"), sem("rw_in")
        w_high, w_low = sem("w_high"), sem("w_low")
        load_in, xt2_ps = [sem("load_in0"), sem("load_in1")], sem("xt2_ps")
        x_high, x_low, meta_taken = sem("x_high"), sem("x_low"), sem("meta_taken")
        tables, table_at, filled, made_tables = sem("tables"), sem("table_at"), sem("filled"), sem("made_tables")
        fill_made, tables_begun = sem("fill_made"), sem("tables_begun")
        gate_ps, up_ps, silu_done, h_done = sem("gate_ps"), sem("up_ps"), sem("silu_done"), sem("h_done")
        y_ps, scaled, result_out = sem("y_ps"), sem("scaled"), [sem("result_out0"), sem("result_out1")]
        final_in = [sem(f"final_in{n}") for n in range(AHEAD)]
        sum_done, acc_done = sem("sum_done"), sem("acc_done")
        stats2_done, mv2_done, ve2_done, rstd2_done, y_done, y_out = (
            sem(n) for n in ("stats2_done", "mv2_done", "ve2_done", "rstd2_done", "y_done", "y_out"))
        N_CONST = 8
        LINKS = 15

        def after(eng, semaphore, count):
            if not isinstance(count, int) or count > 0:
                eng.wait_ge(semaphore, count)

        def settle(eng):
            eng.nop(nofuse=True)

        def there(k):
            return not isinstance(k, int) or k < STEPS

        def all_steps(eng, step):
            step(0, 0, True, False)
            step(1, 1, False, False)
            with eng.Fori(1, STEPS // 2 - 2) as t:
                step(2 * t, 0, False, False)
                step(2 * t + 1, 1, False, False)
            for i in range(STEPS - 4, STEPS):
                step(i, i % 2, False, i == STEPS - 1)

        def scatter(k):
            nc.gpsimd.wait_ge(chain, LINKS * (k + 1))
            settle(nc.gpsimd)
            nc.gpsimd.wait_ge(rows_made, k + 1)
            settle(nc.gpsimd)
            for c in range(TOP):
                for q in range(TT):
                    n = TT * c + q
                    nc.gpsimd.indirect_dma_start(slots, bass.IndirectOffsetOnAxis(ap=slot_at[:, n:n + 1], axis=0),
                                                 rows_sb[:, c, q, :], None).then_inc(scattered, 16)

        with nc.Block() as block:
            @block.sync
            def _(sp):
                for dst, src in ((w_q, wq), (w_k, wk), (w_v, wv), (w_o, wo)):
                    sp.dma_start(dst[:, :], src).then_inc(consts_in, 16)
                for dst, src in ((b_q, bq), (b_k, bk), (b_v, bv)):
                    sp.dma_start(dst[:, :], src.rearrange("(p a) -> p a", a=1)).then_inc(consts_in, 16)
                sp.dma_start(b_o[:, :], bo.rearrange("(a d) -> a d", a=1).to_broadcast([P, DM])).then_inc(consts_in, 16)

                def load(k, par):
                    after(sp, xt_ps, k)
                    settle(sp)
                    after(sp, xb_ready, k - 1)
                    settle(sp)
                    sp.dma_start(x_sb[:, par, :, :], x_steps[k]).then_inc(x_in, 16)

                load(0, 0)
                sp.dma_start(rw_sb[:, :], rw_t).then_inc(rw_in, 16)
                for n, src in ((0, bias), (1, bias_t)):
                    for rows in (0, 64):
                        sp.dma_start(prob[rows:rows + 64, n, :], src).then_inc(bias_in, 16)

                def halves_out(k, par):
                    after(sp, s_stacked, 80 * (k - 1))
                    settle(sp)
                    after(sp, t_stacked, 80 * (k - 1))
                    settle(sp)
                    for n in range(2):
                        sp.wait_ge(halves, 4 * k + 2 * n + 2)
                        settle(sp)
                        for c in range(C):
                            part = c % 2 if n == 0 else c // 2
                            sp.dma_start(scratch[par, n, :, c, :, :], qk_hl[:, n, part, :]).then_inc(scratched, 16)
                    sp.wait_ge(scratched, 16 * 2 * C * (k + 1))
                    settle(sp)

                def stacks(k, par, n, signal):
                    after(sp, signal, 80 * k)
                    settle(sp)
                    if isinstance(k, int) and k < 2:
                        sp.wait_ge(cleared, k + 1)
                        settle(sp)
                    sp.dma_start(stack[:, par, n, :, :],
                                 scratch[par, n].rearrange("j c (d g) t -> (j c d) g t", g=G)).then_inc(signal, 16)
                    for j in range(4):
                        sp.dma_start(blocks[32 * j:32 * j + 32, par, 1 - n, :, j, :],
                                     scratch[par, 1 - n, j].rearrange("c (d g) t -> (c d) g t", g=G)).then_inc(signal, 16)

                def stacks_s(k, par):
                    after(sp, s_ready, NU * (k - 1))
                    settle(sp)
                    stacks(k, par, 0, s_stacked)

                def stacks_t(k, par):
                    after(sp, st_ready, NU * (k - 1))
                    settle(sp)
                    stacks(k, par, 1, t_stacked)

                def weights():
                    sp.dma_start(wgu_sb[:, :, 0:HID], wg.rearrange("e d h -> d e h")).then_inc(w_in, 16)
                    sp.dma_start(wgu_sb[:, :, HID:2 * HID], wu.rearrange("e d h -> d e h")).then_inc(w_in, 16)
                    sp.dma_start(wd_sb[:, :, :, :], wd.rearrange("e (n p) d -> p e n d", p=P)).then_inc(w_in, 16)

                def rows(k):
                    after(sp, st_ready, NU * k)
                    settle(sp)
                    sp.wait_ge(maxt_ready, k + 1)
                    settle(sp)
                    for a in range(2):
                        sp.dma_start(max_rows[a:a + 1, :, :], maxt_sb[:, 64 * a:64 * a + 64]).then_inc(rows_in, 16)

                def store(k, par):
                    sp.wait_ge(x1_done, k + 1)
                    settle(sp)
                    sp.dma_start(x1_steps[k], x1_sb[:, par, :, :]).then_inc(x1_out, 16)

                def step(i, par, first, last):
                    if there(i + 1):
                        stacks_t(i + 1, 1 - par)
                    if there(i + 3):
                        load(i + 3, 1 - par)
                    if not first:
                        store(i - 1, 1 - par)
                    if there(i + 2):
                        halves_out(i + 2, par)
                        stacks_s(i + 2, par)
                    if there(i + 1):
                        rows(i + 1)

                load(1, 1)
                halves_out(0, 0)
                stacks_s(0, 0)
                stacks_t(0, 0)
                load(2, 0)
                halves_out(1, 1)
                stacks_s(1, 1)
                sp.wait_ge(rows_cleared, 1)
                rows(0)
                weights()
                sp.wait_ge(fill_made, 2)
                for n in range(SPARE):
                    at = E * REGION + n * TOK
                    sp.dma_start(slots[at:at + TOK, :].rearrange("(t p) c -> p t c", p=P), fill[:, n, :, :]).then_inc(filled, 16)
                all_steps(sp, step)
                store(STEPS - 1, 1)
                sp.wait_ge(x1_out, 16 * STEPS)

            @block.gpsimd
            def _(pool):
                count = [0]

                def link(ins):
                    count[0] += 1
                    ins.then_inc(made, 1)
                    pool.wait_ge(made, count[0])

                link(pool.memset(ident[:, :], 0.0))
                link(pool.affine_select(out=ident[:, :], in_=ident[:, :], compare_op=ALU.not_equal, fill=1.0, base=0,
                                        pattern=[[-1, P]], channel_multiplier=1))
                link(pool.memset(fold_f[:, :], 0.0))
                for base in (0, 64, -64):
                    link(pool.affine_select(out=fold_f[:, :], in_=fold_f[:, :], compare_op=ALU.not_equal, fill=1.0,
                                            base=base, pattern=[[-1, P]], channel_multiplier=1))
                link(pool.tensor_copy(fold[:, :], fold_f[:, :]))
                link(pool.memset(half[:, :], 1.0))
                link(pool.affine_select(out=half[:, :], in_=half[:, :], compare_op=ALU.is_ge, fill=0.0, base=0,
                                        pattern=[[1, P]], channel_multiplier=-64))
                link(pool.affine_select(out=half[:, :], in_=half[:, :], compare_op=ALU.is_ge, fill=0.0, base=63,
                                        pattern=[[-1, P]], channel_multiplier=64))
                pool.memset(minus_half[:, :], -0.5).then_inc(first_constants, 1)

                def add_bias(k, par):
                    pool.wait_ge(x_in, 16 * (k + 1))
                    after(pool, res_done, k - 1)
                    settle(pool)
                    pool.tensor_tensor(xb_sb[:, par, :, :], x_sb[:, par, :, :],
                                       b_o[:, :].unsqueeze(1).to_broadcast([P, TT, P]), ALU.add).then_inc(xb_ready, 1)

                def split(k):
                    after(pool, scratched, 16 * 2 * C * k)
                    for n in range(2):
                        pool.wait_ge(qk_copied, 2 * k + n + 1)
                        settle(pool)
                        pool.tensor_copy(qk_hl[:, n, 0, :], qk_f[:, n, :]).then_inc(halves, 1)
                        pool.wait_ge(halves, 4 * k + 2 * n + 1)
                        pool.tensor_tensor(qk_hl[:, n, 1, :], qk_f[:, n, :], qk_hl[:, n, 0, :], ALU.subtract).then_inc(halves, 1)

                def norm(k, par):
                    pool.wait_ge(mv_done, k + 1)
                    settle(pool)
                    pool.tensor_scalar(ve[:, :], mean_var[:, :, 1], EPS, None, ALU.add).then_inc(ve_done, 1)
                    pool.wait_ge(ve_done, k + 1)
                    pool.tensor_tensor(rstd[:, :], ve[:, :], minus_half[:, :], ALU.pow).then_inc(rstd_done, 1)
                    pool.wait_ge(rstd_done, k + 1)
                    after(pool, x1_out, 16 * k)
                    settle(pool)
                    for t in range(TT):
                        last = pool.tensor_scalar(x1_sb[:, par, t, :], res[:, t, :], mean_var[:, t, 0:1], rstd[:, t:t + 1],
                                                  ALU.subtract, ALU.mult)
                    last.then_inc(x1_done, 1)

                def powers(k):
                    pool.wait_ge(neg_done, k + 1)
                    settle(pool)
                    pool.tensor_tensor(expo[:, :], euler[:, :], neg_top[:, :], ALU.pow).then_inc(expo_done, 1)

                def step(i, par, first, last):
                    if not first:
                        norm(i - 1, 1 - par)
                    if there(i + 1):
                        add_bias(i + 1, 1 - par)
                    if there(i + 2):
                        split(i + 2)
                    if not first:
                        powers(i - 1)
                        scatter(i - 1)

                pool.wait_ge(first_constants, 1)
                pool.wait_ge(consts_in, 16 * N_CONST)
                split(0)
                for n, shares in enumerate(SHARES):
                    for q in range(4):
                        link(pool.tensor_scalar(diag[32 * q:32 * q + 32, n, :], fold_f[32 * q:32 * q + 32, 0:64],
                                                shares[q % 2], None, ALU.mult))
                link(pool.iota(lane[:, :], pattern=[[1, E]], base=0, channel_multiplier=0,
                               allow_small_or_imprecise_dtypes=True))
                link(pool.iota(counts[:, 1, :], pattern=[[REGION, E]], base=0, channel_multiplier=0,
                               allow_small_or_imprecise_dtypes=True))
                link(pool.memset(ones[:, :], 1.0))
                link(pool.affine_select(out=tri[:, :], in_=ones[:, :], compare_op=ALU.is_gt, fill=0.0, base=0,
                                        pattern=[[1, P]], channel_multiplier=-1))
                link(pool.memset(member[:, :, :], 0.0))
                for c in range(TOP):
                    for q in range(TT):
                        link(pool.iota(rows_sb[:, c, q, DM + 1:DM + 2], pattern=[[0, 1]], base=TOP * P * q + c,
                                       channel_multiplier=TOP, allow_small_or_imprecise_dtypes=True))
                link(pool.memset(v_sb[:, :, :, :, :, :], 0.0))
                for a in range(2):
                    for par in range(2):
                        link(pool.memset(v_sb[64 * a:64 * a + 64, par, :, :, a, D:D + 1], 1.0))
                pool.memset(euler[:, :], EULER).then_inc(constants, 1)
                pool.wait_ge(constants, 1)
                add_bias(0, 0)
                split(1)
                pool.memset(fill[:, :, :, :], 0.0).then_inc(fill_made, 1)
                pool.wait_ge(fill_made, 1)
                pool.iota(fill[:, :, :, DM + 1], pattern=[[TOK, E], [P, TT]], base=TOP * N_TOK + E * TOK, channel_multiplier=1,
                          allow_small_or_imprecise_dtypes=True).then_inc(fill_made, 1)
                all_steps(pool, step)
                norm(STEPS - 1, 1)
                powers(STEPS - 1)
                pool.wait_ge(filled, 16 * SPARE)
                pool.tensor_scalar(fill[:, :, :, DM + 1], fill[:, :, :, DM + 1], -float(E * TOK), None, ALU.add).then_inc(fill_made, 1)

            @block.scalar
            def _(act):
                act.wait_ge(consts_in, 16 * N_CONST)
                act.mul(b_qs[:, :], b_q[:, :], SCALE).then_inc(bqs_ready, 1)
                act.wait_ge(bqs_ready, 1)

                def xt_copy(k, par):
                    act.wait_ge(xt_ps, k + 1)
                    after(act, v_ps, 2 * (k - 1))
                    act.copy(xt_sb[:, par, :], bank[1][:, :]).then_inc(xt_ready, 1)

                def qk_copy(k):
                    for n, (b, s) in enumerate(((b_qs, SCALE), (b_k, 1.0))):
                        act.wait_ge(qk_ps, 2 * k + n + 1)
                        after(act, halves, 4 * k - 2 + 2 * n)
                        act.activation(qk_f[:, n, :], bank[n][:, :], ACT.Identity, bias=b[:, :], scale=s).then_inc(qk_copied, 1)

                def v_copy(k, par, n):
                    u0, u1 = ((0, 4), (4, NU))[n]
                    act.wait_ge(v_ps, 2 * k + n + 1)
                    after(act, pv_done, NU * (k - 1))
                    for a in range(2):
                        rows = slice(64 * a, 64 * a + 64)
                        last = act.copy(v_sb[rows, par, u0:u1, :, a, 0:D],
                                        bank[n][rows, 0:(u1 - u0) * P].rearrange("p (u h d) -> p u h d", h=H, d=D))
                    last.then_inc(v_copied, 1)

                def x1_copy(k, par):
                    act.wait_ge(x1t_ps, k + 1)
                    act.copy(x1t_sb[:, :], bank[1][:, :]).then_inc(x1t_ready, 1)
                    after(act, scattered, 16 * TOP * TT * k)
                    settle(act)
                    for c in range(TOP):
                        last = act.copy(rows_sb[:, c, :, 0:DM], x1_sb[:, par, :, :])
                    last.then_inc(rows_made, 1)

                def ctx_copy(k):
                    act.wait_ge(ctx_done, NU * (k + 1))
                    after(act, wo_ps, k)
                    act.activation(ctxt_sb[:, :], ctx_ps[:, :], ACT.Identity, bias=b_v[:, :], scale=1.0).then_inc(ctxt_ready, 1)

                def step(i, par, first, last):
                    if not first:
                        ctx_copy(i - 1)
                    for u in range(NU):
                        act.wait_ge(st_ready, NU * i + u + 1)
                        after(act, pv_done, NU * i + u - 1)
                        act.activation(prob[:, (par + u) % 2, :], scoret_ps[:, :, :].rearrange("p b c -> p (b c)"),
                                       ACT.Exp).then_inc(exp_done, 1)
                        if u == 0 and there(i + 2):
                            xt_copy(i + 2, par)
                        if u == 1 and there(i + 2):
                            qk_copy(i + 2)
                        if u == 2 and there(i + 1):
                            v_copy(i + 1, 1 - par, 0)
                        if u == 4 and not first:
                            x1_copy(i - 1, 1 - par)
                    if there(i + 1):
                        v_copy(i + 1, 1 - par, 1)

                for k in range(2):
                    xt_copy(k, k)
                    qk_copy(k)
                act.wait_ge(constants, 1)
                v_copy(0, 0, 0)
                v_copy(0, 0, 1)
                all_steps(act, step)
                ctx_copy(STEPS - 1)
                x1_copy(STEPS - 1, 1)

            @block.vector
            def _(dve):
                dve.memset(blocks[:, 0, :, :, :, :], 0.0).then_inc(cleared, 1)
                dve.wait_ge(bias_in, 64)
                dve.tensor_copy(bias_hl[:, :, :], prob[:, :, :]).then_inc(dve_made, 1)
                dve.wait_ge(dve_made, 1)
                dve.tensor_tensor(bias_hl[64:128, :, :], prob[64:128, :, :], bias_hl[64:128, :, :],
                                  ALU.subtract).then_inc(dve_made, 1)
                dve.memset(max_rows[:, :, :], 0.0).then_inc(rows_cleared, 1)
                dve.memset(blocks[:, 1, :, :, :, :], 0.0).then_inc(cleared, 1)

                def maximum(k, par, v, ps=score_ps):
                    dve.wait_ge(s_ready, NU * k + v + 1)
                    dve.tensor_reduce(neg_max[:, par, v, :], ps[:, :, :].rearrange("p b (h k) -> p (b h) k", k=W),
                                      AX_X, ALU.max, negate=True).then_inc(max_done, 1)

                def max_copy(k):
                    dve.wait_ge(maxt_ps, k + 1)
                    after(dve, rows_in, 32 * k)
                    dve.tensor_copy(maxt_sb[:, :], bank[0][0:NU * H, 0:P]).then_inc(maxt_ready, 1)

                def normalise(i, par, u):
                    n = NU * i + u
                    dve.wait_ge(pv_done, n + 1)
                    o = o_ps[:, 0:288].rearrange("p (h e a d) -> p h e a d", h=8, e=2, a=2)
                    for e in range(2):
                        rows = slice(64 * e, 64 * e + 64)
                        dve.reciprocal(recip[rows, :, :], o[rows, :, e, :, D]).then_inc(recip_done, 1)
                    dve.wait_ge(recip_done, 2 * n + 2)
                    after(dve, ctx_done, n - 1)
                    for e in range(2):
                        rows = slice(64 * e, 64 * e + 64)
                        last = dve.tensor_tensor(o_sb[rows, (par + u) % 2, :, :, :].rearrange("p a h d -> p h a d"),
                                                 o[rows, :, e, :, 0:D],
                                                 recip[rows, :, :].unsqueeze(3).to_broadcast([64, 8, 2, D]), ALU.mult)
                    last.then_inc(norm_done, 1)

                def residual(k, par):
                    dve.wait_ge(wo_ps, k + 1)
                    dve.wait_ge(xb_ready, k + 1)
                    after(dve, x1_done, k)
                    dve.tensor_tensor(res[:, :, :], bank[0][:, :].rearrange("p (t d) -> p t d", t=TT), xb_sb[:, par, :, :],
                                      ALU.add).then_inc(res_done, 1)
                    dve.wait_ge(res_done, k + 1)
                    for t in range(TT):
                        last = dve.bn_stats(stats[:, t, :], res[:, t, :])
                    last.then_inc(stats_done, 1)
                    dve.wait_ge(stats_done, k + 1)
                    settle(dve)
                    for t in range(TT):
                        last = dve.bn_aggr(mean_var[:, t, :], stats[:, t, :])
                    last.then_inc(mv_done, 1)

                def link(ins, k, n):
                    ins.then_inc(chain, 1)
                    dve.wait_ge(chain, LINKS * k + n)
                    settle(dve)

                def top_two(k):
                    dve.wait_ge(logit_ps, k + 1)
                    settle(dve)
                    link(dve.tensor_copy(logit[:, :, :], bank[1][:, 0:TT * E].rearrange("p (t e) -> p t e", t=TT)), k, 1)
                    for t in range(TT):
                        last = dve.max(top[:, t, :], logit[:, t, :])
                    link(last, k, 2)
                    dve.tensor_scalar(neg_top[:, :].rearrange("p (t c) -> p t c", t=TT), top[:, :, 0:TOP], -1.0, None,
                                      ALU.mult).then_inc(neg_done, 1)
                    for t in range(TT):
                        last = dve.max_index(top_at[:, t, :], top[:, t, :], logit[:, t, :])
                    link(last, k, 3)
                    link(dve.tensor_copy(top_f[:, :, :], top_at[:, :, 0:TOP]), k, 4)
                    for c in range(TOP):
                        last = dve.tensor_tensor(pick[:, c, :, :], lane[:, :].unsqueeze(1).to_broadcast([P, TT, E]),
                                                 top_f[:, :, c:c + 1].to_broadcast([P, TT, E]), ALU.is_equal)
                    link(last, k, 5)
                    link(dve.tensor_tensor(member[:, 0:TT, :], pick[:, 0, :, :], pick[:, 1, :, :], ALU.add), k, 6)

                def gates(k):
                    dve.wait_ge(expo_done, k + 1)
                    settle(dve)
                    link(dve.tensor_scalar(expo1[:, :], expo[:, :], 1.0, None, ALU.add), k, 7)
                    link(dve.reciprocal(gate2[:, :, :].rearrange("p t c -> p (t c)"), expo1[:, :]), k, 8)
                    link(dve.scalar_tensor_tensor(out=gsum[:, :], in0=gate2[:, :, 0], scalar=1e-10, in1=gate2[:, :, 1],
                                                  op0=ALU.add, op1=ALU.add), k, 9)
                    link(dve.reciprocal(ginv[:, :], gsum[:, :]), k, 10)
                    after(dve, scattered, 16 * TOP * TT * k)
                    settle(dve)
                    last = dve.tensor_tensor(rows_sb[:, :, :, DM], gate2[:, :, :].rearrange("p t c -> p c t"),
                                             ginv[:, :].unsqueeze(1).to_broadcast([P, TOP, TT]), ALU.mult)
                    if not (isinstance(k, int) and k == 0):
                        last = dve.tensor_scalar(rows_sb[:, :, :, DM + 1], rows_sb[:, :, :, DM + 1], float(TOP * TOK), None,
                                                 ALU.add)
                    link(last, k, 11)

                def places(k, par):
                    dve.wait_ge(rank_ps, k + 1)
                    settle(dve)
                    ranks = bank[0][:, 256:256 + (TT + 1) * E].rearrange("p (t e) -> p t e", t=TT + 1)
                    dve.tensor_tensor(slot_of[:, :, :], ranks[:, 0:TT, :],
                                      counts[:, 1 - par, :].unsqueeze(1).to_broadcast([P, TT, E]), ALU.add)
                    link(dve.tensor_tensor(counts[:, par, :], ranks[:, TT, :], counts[:, 1 - par, :], ALU.add), k, 12)
                    for c in range(TOP):
                        last = dve.tensor_tensor(picked[:, c, :, :], pick[:, c, :, :], slot_of[:, :, :], ALU.mult)
                    link(last, k, 13)
                    link(dve.tensor_reduce(slot_f[:, :], picked[:, :, :, :].rearrange("p c t e -> p (c t) e"), AX_X, ALU.add),
                         k, 14)
                    link(dve.tensor_copy(slot_at[:, :], slot_f[:, :]), k, 15)

                def step(i, par, first, last):
                    for u in range(TURNS):
                        if there(i + 1):
                            if u < NU:
                                maximum(i + 1, 1 - par, u)
                            if u == NU:
                                max_copy(i + 1)
                        if u == 0 and not first:
                            residual(i - 1, 1 - par)
                        if u == 7 and not first:
                            gates(i - 1)
                        if 1 <= u <= NU:
                            normalise(i, par, u - 1)
                        if u == 5 and not first:
                            top_two(i - 1)
                        if u == 8 and not first:
                            places(i - 1, 1 - par)

                for v in range(NU):
                    maximum(0, 0, v, (score_ps, scoret_ps)[v % 2])
                max_copy(0)
                all_steps(dve, step)
                residual(STEPS - 1, 1)
                top_two(STEPS - 1)
                gates(STEPS - 1)
                places(STEPS - 1, 1)
                dve.tensor_copy(fill_at[:, :], counts[:, (STEPS - 1) % 2, :]).then_inc(tables_begun, 1)
                dve.wait_ge(tables_begun, 1)

            @block.tensor
            def _(pe):
                pe.wait_ge(consts_in, 16 * N_CONST)
                pe.wait_ge(first_constants, 1)
                pe.wait_ge(rw_in, 16)

                def turn_x(k, par):
                    pe.wait_ge(x_in, 16 * (k + 1))
                    after(pe, qk_copied, 2 * k)
                    after(pe, v_copied, 2 * (k - 1))
                    for t in range(TT):
                        last = pe.transpose(bank[1][:, t * P:(t + 1) * P], x_sb[:, par, t, :], ident[:, :])
                    last.then_inc(xt_ps, 1)

                def project_qk(k, par):
                    after(pe, maxt_ready, k - 1)
                    after(pe, res_done, k - 2)
                    pe.wait_ge(xt_ready, k + 1)
                    for n, w in enumerate((w_q, w_k)):
                        pe.matmul(bank[n][:, :], w[:, :], xt_sb[:, par, :], start=True, stop=True).then_inc(qk_ps, 1)

                def turn_x1(k, par):
                    pe.wait_ge(x1_done, k + 1)
                    if there(k + 3):
                        pe.wait_ge(qk_copied, 2 * (k + 4))
                    else:
                        pe.wait_ge(v_copied, min(2 * (k + 2), 2 * STEPS))
                    for t in range(TT):
                        last = pe.transpose(bank[1][:, t * P:(t + 1) * P], x1_sb[:, par, t, :], ident[:, :])
                    last.then_inc(x1t_ps, 1)

                def logits(k):
                    pe.wait_ge(x1t_ready, k + 1)
                    for t in range(TT):
                        last = pe.matmul(bank[1][:, t * E:(t + 1) * E], x1t_sb[:, t * P:(t + 1) * P], rw_sb[:, :],
                                         start=True, stop=True)
                    last.then_inc(logit_ps, 1)

                def ranks(k):
                    pe.wait_ge(chain, LINKS * k + 6)
                    pe.wait_ge(res_done, k + 1)
                    if there(k + 2):
                        pe.wait_ge(maxt_ready, k + 3)
                    width = (TT + 1) * E
                    m = member[:, :, :].rearrange("p t e -> p (t e)")
                    pe.matmul(bank[0][:, 256:256 + width], tri[:, :], m, start=True, stop=False, skip_group_check=True)
                    for b in range(1, TT + 1):
                        last = pe.matmul(bank[0][:, 256 + b * E:256 + width], ones[:, :], m[:, 0:width - b * E],
                                         start=False, stop=True, skip_group_check=True)
                    last.then_inc(rank_ps, 1)

                def project_v(k, par, n):
                    if n == 1 and not (isinstance(k, int) and k < 2):
                        pe.wait_ge(chain, LINKS * (k - 2) + 1)
                    if isinstance(k, int) and k == STEPS - 1:
                        if n == 0:
                            pe.wait_ge(res_done, k - 1)
                        else:
                            pe.wait_ge(v_copied, 2 * k)
                    else:
                        pe.wait_ge(qk_copied, 2 * (k + 1) + n + 1)
                    u0, u1 = ((0, 4), (4, NU))[n]
                    for u in range(u0, u1):
                        a, b = UNITS[u]
                        cols = slice((u - u0) * P, (u - u0 + 1) * P)
                        if b == a + W:
                            last = pe.matmul(bank[n][:, cols], xt_sb[:, par, a:a + P], w_v[:, :], start=True, stop=True)
                        else:
                            for r, t0 in ((0, a), (W, b)):
                                last = pe.matmul(bank[n][r:r + W, cols], xt_sb[:, par, t0:t0 + W], w_v[:, :],
                                                 start=True, stop=True)
                    last.then_inc(v_ps, 1)

                def products(ps, par, u, a_of, b_of):
                    for g in range(G):
                        for a in range(2):
                            t0 = UNITS[u][a]
                            last = pe.matmul(ps[64 * a:64 * a + 64, g // 2, (g % 2) * 4 * W:(g % 2 + 1) * 4 * W],
                                             stack[:, par, a_of, g, t0:t0 + W],
                                             blocks[:, par, b_of, g, :, t0:t0 + W],
                                             start=False, stop=True, skip_group_check=True)
                    return last

                def bias_s(k, v, ps=score_ps, behind=0):
                    after(pe, max_done, NU * k + v - behind)
                    for n in range(2):
                        pe.matmul(ps[:, n, :], fold[:, :], bias_hl[:, 0, n * 512:n * 512 + 512],
                                  start=True, stop=False, skip_group_check=True)

                def bias_t(i, u):
                    after(pe, exp_done, NU * i + u)
                    for n in range(2):
                        pe.matmul(scoret_ps[:, n, :], fold[:, :], bias_hl[:, 1, n * 512:n * 512 + 512],
                                  start=True, stop=False, skip_group_check=True)

                def scores(k, par, v, ps=score_ps):
                    if v == 0:
                        pe.wait_ge(s_stacked, 80 * (k + 1))
                    products(ps, par, v, 0, 1).then_inc(s_ready, 1)

                def scores_t(i, par, u):
                    if u == 0:
                        pe.wait_ge(t_stacked, 80 * (i + 1))
                        pe.wait_ge(rows_in, 32 * (i + 1))
                    for n in range(2):
                        pe.matmul(scoret_ps[:, n, :], half[:, :],
                                  max_rows[:, u * H + 8 * n:u * H + 8 * n + 8, :].rearrange("a h q -> a (h q)"),
                                  start=False, stop=False, skip_group_check=True)
                    products(scoret_ps, par, u, 1, 0).then_inc(st_ready, 1)

                def values(i, par, u):
                    n = NU * i + u
                    pe.wait_ge(exp_done, n + 1)
                    if u == 0:
                        pe.wait_ge(v_copied, 2 * (i + 1))
                    after(pe, norm_done, n)
                    for h in range(8):
                        last = pe.matmul(o_ps[:, h * 36:h * 36 + 36], prob[:, (par + u) % 2, h * P:(h + 1) * P],
                                         v_sb[:, par, u, 2 * h:2 * h + 2, :, :].rearrange("p h a d -> p (h a d)"),
                                         start=True, stop=True)
                    last.then_inc(pv_done, 1)

                def context(i, par, u):
                    pe.wait_ge(norm_done, NU * i + u + 1)
                    if u == 0:
                        after(pe, ctxt_ready, i)
                    settle(pe)
                    for a in range(2):
                        t0 = UNITS[u][a]
                        for e in range(2):
                            rows = slice(64 * e, 64 * e + 64)
                            last = pe.matmul(ctx_ps[rows, t0:t0 + W],
                                             o_sb[rows, (par + u) % 2, a, :, :].rearrange("p h d -> p (h d)"),
                                             diag[rows, share(t0), :], start=(u == 0 and a == 0), stop=(u == NU - 1),
                                             skip_group_check=True)
                    last.then_inc(ctx_done, 1)

                def project_out(k):
                    pe.wait_ge(ctxt_ready, k + 1)
                    if there(k + 1):
                        pe.wait_ge(maxt_ready, k + 2)
                    after(pe, chain, LINKS * (k - 1) + 12)
                    for t in range(TT):
                        last = pe.matmul(bank[0][:, t * P:(t + 1) * P], ctxt_sb[:, t * P:(t + 1) * P], w_o[:, :],
                                         start=True, stop=True)
                    last.then_inc(wo_ps, 1)

                def turn_maxima(k, par):
                    pe.wait_ge(max_done, NU * (k + 1))
                    pe.wait_ge(v_copied, 2 * k + 1)
                    pe.transpose(bank[0][0:NU * H, 0:P], neg_max[:, par, :, :].rearrange("p u h -> p (u h)"),
                                 ident[:, :]).then_inc(maxt_ps, 1)

                def step(i, par, first, last):
                    for u in range(TURNS):
                        if u < NU:
                            if u or first:
                                bias_t(i, u)
                            scores_t(i, par, u)
                            if there(i + 1):
                                if u or first:
                                    bias_s(i + 1, u)
                                scores(i + 1, 1 - par, u)
                        if u == 0:
                            if not first:
                                project_out(i - 1)
                            if there(i + 2):
                                turn_x(i + 2, par)
                        if u == NU and there(i + 1):
                            turn_maxima(i + 1, 1 - par)
                            project_v(i + 1, 1 - par, 1)
                        if u == NU + 1:
                            if there(i + 1):
                                bias_t(i + 1, 0)
                            if there(i + 2):
                                bias_s(i + 2, 0)
                        if u >= 2:
                            context(i, par, u - 2)
                        if 1 <= u <= NU:
                            values(i, par, u - 1)
                        if u == 1 and there(i + 2):
                            project_qk(i + 2, par)
                        if u == 2 and there(i + 1):
                            project_v(i + 1, 1 - par, 0)
                        if not first:
                            if u == 4:
                                turn_x1(i - 1, 1 - par)
                            if u == 5:
                                logits(i - 1)
                            if u == 7:
                                ranks(i - 1)

                for k in range(2):
                    turn_x(k, k)
                    project_qk(k, k)
                project_v(0, 0, 0)
                project_v(0, 0, 1)
                pe.wait_ge(dve_made, 2)
                for v in range(NU):
                    bias_s(0, v, (score_ps, scoret_ps)[v % 2], 1)
                    scores(0, 0, v, (score_ps, scoret_ps)[v % 2])
                turn_maxima(0, 0)
                pe.wait_ge(constants, 1)
                all_steps(pe, step)
                project_out(STEPS - 1)
                turn_x1(STEPS - 1, 1)
                logits(STEPS - 1)
                ranks(STEPS - 1)

        attention.close()

        def sb(name, shape, dt=F32):
            return ctx.enter_context(nc.sbuf_tensor(name, shape, dt))

        wgu_hi = sb("wgu_hi", [P, 2, 2 * HID], F32R)
        wgu_lo = sb("wgu_lo", [P, 2, 2 * HID], F32R)
        taken = sb("taken", [P, E])
        region = sb("region", [P, E])
        marks = sb("marks", [P, E, CHUNKS])
        over = sb("over", [P, E, CHUNKS])
        chunks_of = sb("chunks_of", [P, E])
        upto = sb("upto", [P, E, E])
        summed = sb("summed", [P, E, E])
        cum = sb("cum", [P, E])
        jump = sb("jump", [P, E])
        number = sb("number", [P, SLOT_CHUNKS, E])
        past = sb("past", [P, SLOT_CHUNKS, E])
        jumps = sb("jumps", [P, SLOT_CHUNKS, E])
        expert_f, first_f, used, unused, spare_at, at_f = (sb(n, [P, SLOT_CHUNKS]) for n in
                                                            ("expert_f", "first_f", "used", "unused", "spare_at", "at_f"))
        expert_at, first_at = sb("expert_at", [P, SLOT_CHUNKS], I32), sb("first_at", [P, SLOT_CHUNKS], I32)
        xin = sb("xin", [P, 2, TT, ROW])
        x_hi, x_lo = sb("x_hi", [P, 2, TOK], F32R), sb("x_lo", [P, 2, TOK], F32R)
        meta = sb("meta", [P, 2, TT, 2])
        silu_sb = sb("silu_sb", [P, 2, TOK])
        h_sb = sb("h_sb", [P, 2, 2, TOK])
        scaled_sb = sb("scaled_sb", [P, 2, TT, DM])
        result_at = [sb(f"result_at{n}", [P, TT], U32) for n in range(2)]

        with nc.Block() as block:
            def table_value(eng, table, s, largest):
                at = table[0:1, s:s + 1] if isinstance(s, int) else table[0:1, bass.ds(s, 1)]
                return eng.value_load(at, min_val=0, max_val=largest)

            def all_chunks(eng, chunk):
                chunk(0, 0, 0)
                chunk(1, 1, 0)
                pairs = (SLOT_CHUNKS - 3) // 2
                with eng.Fori(1, pairs) as t:
                    chunk(2 * t, 0, t)
                    chunk(2 * t + 1, 1, t)
                for s in range(2 * pairs, SLOT_CHUNKS):
                    chunk(s, s % 2, s // 2)

            @block.sync
            def _(sp):
                sp.wait_ge(fill_made, 3)
                for e in range(0, E, 2):
                    at = sp.value_load(fill_at[0:1, e:e + 1], min_val=REGION * e, max_val=REGION * e + N_TOK)
                    sp.dma_start(slots[bass.ds(at, TOK), :].rearrange("(t p) c -> p t c", p=P),
                                 fill[:, e, :, :]).then_inc(filled, 16)
                sp.wait_ge(filled, 16 * (SPARE + E))
                sp.wait_ge(scattered, 16 * TOP * TT * STEPS)
                sp.wait_ge(tables, 1)

                def load(s, par):
                    after(sp, xt2_ps, s - 1)
                    settle(sp)
                    after(sp, meta_taken, s - 1)
                    settle(sp)
                    at = table_value(sp, first_at, s, E * REGION + (SPARE - 1) * TOK)
                    sp.dma_start(xin[:, par, :, :],
                                 slots[bass.ds(at, TOK), :].rearrange("(t p) c -> p t c", p=P)).then_inc(load_in[par], 16)

                def chunk(s, par, pair):
                    load(s, par)

                all_chunks(sp, chunk)

            @block.gpsimd
            def _(pool):
                pool.iota(region[:, :], pattern=[[REGION, E]], base=0, channel_multiplier=0,
                          allow_small_or_imprecise_dtypes=True).then_inc(table_at, 1)
                pool.iota(marks[:, :, :], pattern=[[0, E], [TOK, CHUNKS]], base=0, channel_multiplier=0,
                          allow_small_or_imprecise_dtypes=True).then_inc(table_at, 1)
                pool.iota(upto[:, :, :], pattern=[[1, E], [-1, E]], base=0, channel_multiplier=0,
                          allow_small_or_imprecise_dtypes=True).then_inc(table_at, 1)
                pool.iota(number[:, :, :], pattern=[[1, SLOT_CHUNKS], [0, E]], base=0, channel_multiplier=0,
                          allow_small_or_imprecise_dtypes=True).then_inc(table_at, 1)
                scatter(STEPS - 1)

                def chunk(s, par, pair):
                    pool.wait_ge(scaled, s + 1)
                    settle(pool)
                    for t in range(TT):
                        pool.indirect_dma_start(results, bass.IndirectOffsetOnAxis(ap=result_at[par][:, t:t + 1], axis=0),
                                                scaled_sb[:, par, t, :], None).then_inc(result_out[par], 16)

                all_chunks(pool, chunk)
                for par in range(2):
                    pool.wait_ge(result_out[par], 16 * TT * ((SLOT_CHUNKS + 1 - par) // 2))

            @block.scalar
            def _(act):
                def high(s, par):
                    act.wait_ge(xt2_ps, s + 1)
                    after(act, up_ps, 2 * (s - 1))
                    settle(act)
                    act.copy(x_hi[:, par, :], bank[par][:, :]).then_inc(x_high, 1)

                def weights_high(s, par):
                    e = table_value(act, expert_at, s, E - 1)
                    after(act, up_ps, 2 * (s - 1))
                    settle(act)
                    act.copy(wgu_hi[:, par, :], wgu_sb[:, e, :]).then_inc(w_high, 1)

                def silu(s, hh):
                    act.wait_ge(gate_ps, 2 * s + hh + 1)
                    after(act, h_done, 2 * s + hh - 1)
                    act.activation(silu_sb[:, hh, :], (score_ps, scoret_ps)[hh][:, 0, :], ACT.Silu).then_inc(silu_done, 1)

                def chunk(s, par, pair):
                    silu(s, 0)
                    if not (isinstance(s, int) and s == SLOT_CHUNKS - 1):
                        weights_high(s + 1, 1 - par)
                        high(s + 1, 1 - par)
                    silu(s, 1)

                for e in range(1, E, 2):
                    at = act.value_load(fill_at[0:1, e:e + 1], min_val=REGION * e, max_val=REGION * e + N_TOK)
                    act.dma_start(slots[bass.ds(at, TOK), :].rearrange("(t p) c -> p t c", p=P),
                                  fill[:, e, :, :]).then_inc(filled, 16)
                act.wait_ge(w_in, 48)
                act.wait_ge(tables, 1)
                weights_high(0, 0)
                high(0, 0)
                all_chunks(act, chunk)

            @block.vector
            def _(dve):
                done = [0]

                def link(ins):
                    done[0] += 1
                    ins.then_inc(made_tables, 1)
                    dve.wait_ge(made_tables, done[0])

                total = counts[:, (STEPS - 1) % 2, :]
                dve.wait_ge(table_at, 4)
                link(dve.tensor_tensor(taken[:, :], total, region[:, :], ALU.subtract))
                link(dve.tensor_tensor(over[:, :, :], taken[:, :].unsqueeze(2).to_broadcast([P, E, CHUNKS]), marks[:, :, :],
                                       ALU.is_gt))
                link(dve.tensor_reduce(chunks_of[:, :], over[:, :, :], AX_X, ALU.add))
                link(dve.tensor_scalar(upto[:, :, :], upto[:, :, :], 0.0, None, ALU.is_ge))
                link(dve.tensor_tensor(summed[:, :, :], upto[:, :, :], chunks_of[:, :].unsqueeze(1).to_broadcast([P, E, E]),
                                       ALU.mult))
                link(dve.tensor_reduce(cum[:, :], summed[:, :, :], AX_X, ALU.add))
                link(dve.tensor_scalar(jump[:, :], chunks_of[:, :], -float(TOK), float(REGION), ALU.mult, ALU.add))
                link(dve.tensor_tensor(past[:, :, :], number[:, :, :],
                                       cum[:, :].unsqueeze(1).to_broadcast([P, SLOT_CHUNKS, E]), ALU.is_ge))
                link(dve.tensor_reduce(expert_f[:, :], past[:, :, :], AX_X, ALU.add))
                link(dve.tensor_tensor(jumps[:, :, :], past[:, :, :],
                                       jump[:, :].unsqueeze(1).to_broadcast([P, SLOT_CHUNKS, E]), ALU.mult))
                link(dve.tensor_reduce(first_f[:, :], jumps[:, :, :], AX_X, ALU.add))
                link(dve.scalar_tensor_tensor(out=at_f[:, :], in0=number[:, :, 0], scalar=float(TOK), in1=first_f[:, :],
                                              op0=ALU.mult, op1=ALU.add))
                link(dve.tensor_scalar(used[:, :], expert_f[:, :], float(E), None, ALU.is_lt))
                link(dve.tensor_tensor(expert_f[:, :], expert_f[:, :], used[:, :], ALU.mult))
                dve.tensor_scalar(spare_at[:, :], number[:, :, 0], float(TOK), float(E * REGION - FULL * TOK), ALU.mult,
                                  ALU.add)
                link(dve.tensor_scalar(unused[:, :], used[:, :], -1.0, 1.0, ALU.mult, ALU.add))
                dve.tensor_tensor(first_f[:, :], at_f[:, :], used[:, :], ALU.mult)
                link(dve.tensor_tensor(spare_at[:, :], spare_at[:, :], unused[:, :], ALU.mult))
                link(dve.tensor_tensor(at_f[:, :], first_f[:, :], spare_at[:, :], ALU.add))
                link(dve.tensor_copy(expert_at[:, :], expert_f[:, :]))
                dve.tensor_copy(first_at[:, :], at_f[:, :]).then_inc(tables, 1)
                dve.wait_ge(tables, 1)

                def weights_low(s, par):
                    e = table_value(dve, expert_at, s, E - 1)
                    dve.wait_ge(w_high, s + 1)
                    after(dve, up_ps, 2 * (s - 1))
                    settle(dve)
                    dve.tensor_tensor(wgu_lo[:, par, :], wgu_sb[:, e, :], wgu_hi[:, par, :].bitcast(F32),
                                      ALU.subtract).then_inc(w_low, 1)

                def low(s, par):
                    dve.wait_ge(x_high, s + 1)
                    after(dve, up_ps, 2 * (s - 1))
                    settle(dve)
                    dve.tensor_tensor(x_lo[:, par, :], bank[par][:, :], x_hi[:, par, :].bitcast(F32),
                                      ALU.subtract).then_inc(x_low, 1)

                def hidden(s, b, hh):
                    dve.wait_ge(silu_done, 2 * s + hh + 1)
                    dve.wait_ge(up_ps, 2 * s + hh + 1)
                    after(dve, y_ps, s - 1)
                    dve.tensor_tensor(h_sb[:, b, hh, :], silu_sb[:, hh, :], (score_ps, scoret_ps)[hh][:, 1, :],
                                      ALU.mult).then_inc(h_done, 1)

                def scale(s, par, pair):
                    dve.wait_ge(y_ps, s + 1)
                    after(dve, result_out[par], 16 * TT * pair)
                    settle(dve)
                    y = (o_ps, ctx_ps)[par]
                    dve.wait_ge(meta_taken, s + 1)
                    settle(dve)
                    dve.tensor_copy(result_at[par][:, :], meta[:, par, :, 1])
                    for t in range(TT):
                        last = dve.tensor_scalar(scaled_sb[:, par, t, :], y[:, t * P:(t + 1) * P],
                                                 meta[:, par, t, 0:1], None, ALU.mult)
                    last.then_inc(scaled, 1)

                def chunk(s, par, pair):
                    after(dve, scaled, s - 1)
                    settle(dve)
                    dve.tensor_copy(meta[:, par, :, :], xin[:, par, :, DM:ROW]).then_inc(meta_taken, 1)
                    hidden(s, par, 0)
                    if not (isinstance(s, int) and s == SLOT_CHUNKS - 1):
                        weights_low(s + 1, 1 - par)
                        low(s + 1, 1 - par)
                    hidden(s, par, 1)
                    if not (isinstance(s, int) and s == 0):
                        scale(s - 1, 1 - par, pair - 1 + par)

                weights_low(0, 0)
                low(0, 0)
                all_chunks(dve, chunk)
                scale(SLOT_CHUNKS - 1, (SLOT_CHUNKS - 1) % 2, (SLOT_CHUNKS - 1) // 2)

            @block.tensor
            def _(pe):
                pe.wait_ge(w_in, 48)
                pe.wait_ge(tables, 1)

                def turn(s, par, t):
                    pe.wait_ge(load_in[par], 16 * (t + 1))
                    after(pe, x_low, s - 1)
                    for q in range(TT):
                        last = pe.transpose(bank[par][:, q * P:(q + 1) * P], xin[:, par, q, 0:DM], ident[:, :])
                    last.then_inc(xt2_ps, 1)

                def gate_up(s, par, hh):
                    after(pe, h_done, 2 * s + hh - 1)
                    if hh == 0:
                        pe.wait_ge(x_low, s + 1)
                        pe.wait_ge(w_low, s + 1)
                    for n, signal in ((0, gate_ps), (1, up_ps)):
                        cols = slice(n * HID + hh * P, n * HID + hh * P + P)
                        out_ps = (score_ps, scoret_ps)[hh][:, n, :]
                        pe.matmul(out_ps, wgu_hi[:, par, cols], x_lo[:, par, :], start=True, stop=False)
                        pe.matmul(out_ps, wgu_lo[:, par, cols], x_hi[:, par, :], start=False, stop=False)
                        pe.matmul(out_ps, wgu_hi[:, par, cols], x_hi[:, par, :], start=False, stop=True).then_inc(signal, 1)

                def down(s, par):
                    e = table_value(pe, expert_at, s, E - 1)
                    pe.wait_ge(h_done, 2 * s + 2)
                    after(pe, scaled, s - 1)
                    y = (o_ps, ctx_ps)[par]
                    for t in range(TT):
                        cols = slice(t * P, (t + 1) * P)
                        for c in range(2):
                            last = pe.matmul(y[:, cols], h_sb[:, par, c, cols], wd_sb[:, e, c, :],
                                             start=(c == 0), stop=(c == 1))
                    last.then_inc(y_ps, 1)

                def chunk(s, par, pair):
                    gate_up(s, par, 0)
                    if not (isinstance(s, int) and s == SLOT_CHUNKS - 1):
                        turn(s + 1, 1 - par, pair + par)
                    gate_up(s, par, 1)
                    if not (isinstance(s, int) and s == 0):
                        down(s - 1, 1 - par)

                turn(0, 0, 0)
                all_chunks(pe, chunk)
                down(SLOT_CHUNKS - 1, (SLOT_CHUNKS - 1) % 2)

        final_x = sb("final_x", [P, AHEAD, TT, DM])
        final_y = sb("final_y", [P, AHEAD, TT, TOP, DM])
        total_sb = sb("total_sb", [P, AHEAD, TT, DM])
        stats2, mv2 = sb("stats2", [P, TT, 6]), sb("mv2", [P, 2, TT, 2])
        ve2, rstd2 = sb("ve2", [P, TT]), sb("rstd2", [P, 2, TT])
        y_sb = sb("y_sb", [P, 2, TT, DM])

        with nc.Block() as block:
            @block.sync
            def _(sp):
                def load(k, par):
                    after(sp, acc_done, k + 1 - AHEAD)
                    sp.dma_start(final_x[:, par, :, :], x1_steps[k]).then_inc(final_in[par], 16)
                    sp.dma_start(final_y[:, par, :, :, :], results_steps[k]).then_inc(final_in[par], 16)

                for k in range(CHUNKS):
                    load(k, k % AHEAD)

            @block.gpsimd
            def _(pool):
                def choices(k, buf):
                    pool.wait_ge(final_in[buf], 32 * (k // AHEAD + 1))
                    after(pool, y_done, k + 1 - AHEAD)
                    pool.tensor_tensor(total_sb[:, buf, :, :], final_y[:, buf, :, 0, :], final_y[:, buf, :, 1, :],
                                       ALU.add).then_inc(sum_done, 1)

                choices(0, 0)
                for k in range(CHUNKS):
                    if k + 1 < CHUNKS:
                        choices(k + 1, (k + 1) % AHEAD)
                    after(pool, rstd2_done, k)
                    pool.wait_ge(mv2_done, k + 1)
                    pool.tensor_scalar(ve2[:, :], mv2[:, k % 2, :, 1], EPS, None, ALU.add).then_inc(ve2_done, 1)
                    pool.wait_ge(ve2_done, k + 1)
                    after(pool, y_done, k - 1)
                    pool.tensor_tensor(rstd2[:, k % 2, :], ve2[:, :], minus_half[:, :], ALU.pow).then_inc(rstd2_done, 1)

            @block.scalar
            def _(act):
                for k in range(CHUNKS):
                    act.wait_ge(y_done, k + 1)
                    after(act, y_out, 16 * k)
                    act.dma_start(out_steps[k], y_sb[:, k % 2, :, :]).then_inc(y_out, 16)
                act.wait_ge(y_out, 16 * CHUNKS)

            @block.vector
            def _(dve):
                def normalise_out(k, par):
                    buf = k % AHEAD
                    dve.wait_ge(rstd2_done, k + 1)
                    after(dve, y_out, 16 * (k - 1))
                    for t in range(TT):
                        last = dve.tensor_scalar(y_sb[:, par, t, :], total_sb[:, buf, t, :], mv2[:, par, t, 0:1],
                                                 rstd2[:, par, t:t + 1], ALU.subtract, ALU.mult)
                    last.then_inc(y_done, 1)

                for k in range(CHUNKS):
                    par, buf = k % 2, k % AHEAD
                    dve.wait_ge(sum_done, k + 1)
                    dve.tensor_tensor(total_sb[:, buf, :, :], total_sb[:, buf, :, :], final_x[:, buf, :, :],
                                      ALU.add).then_inc(acc_done, 1)
                    dve.wait_ge(acc_done, k + 1)
                    for t in range(TT):
                        last = dve.bn_stats(stats2[:, t, :], total_sb[:, buf, t, :])
                    last.then_inc(stats2_done, 1)
                    dve.wait_ge(stats2_done, k + 1)
                    after(dve, y_done, k - 1)
                    for t in range(TT):
                        last = dve.bn_aggr(mv2[:, par, t, :], stats2[:, t, :])
                    last.then_inc(mv2_done, 1)
                    if k:
                        normalise_out(k - 1, 1 - par)
                normalise_out(CHUNKS - 1, (CHUNKS - 1) % 2)


def kernel(**inputs):
    import numpy as np
    import concourse.bacc as bacc
    from concourse import mybir as mb
    from concourse.bass_utils import run_bass_kernel_spmd

    a = {n.replace("L0_attn_", "").replace("L0_ffn_", ""): np.asarray(v) for n, v in inputs.items()}
    qk = np.array([8 * (4 * g + j) + d for j in range(4) for d in range(D) for g in range(G)])
    order = np.empty(H, int)
    for j in range(4):
        for g in range(G):
            order[place(j, g)] = 4 * g + j
    vals = np.array([8 * h + d for h in order for d in range(D)])
    turned = np.array([8 * h + d for h in np.concatenate([order[0::2], order[1::2]]) for d in range(D)])
    bias = a["pos_bias"][order]
    arrays = {
        "x": a["hidden_states"], "wq": a["Wq"][:, qk], "bq": a["bq"][qk], "wk": a["Wk"][:, qk], "bk": a["bk"][qk],
        "wv": a["Wv"][:, vals], "bv": a["bv"][turned], "wo": a["Wo"][turned], "bo": a["bo"],
        "bias": bias.transpose(1, 0, 2).reshape(W, H * W), "bias_t": bias.transpose(2, 0, 1).reshape(W, H * W),
        "rw_t": a["router_w"].T, "wg": a["w_gate"], "wu": a["w_up"], "wd": a["w_down"],
    }
    nc = bacc.Bacc("TRN2", target_bir_lowering=False, num_devices=1)
    feeds, args = {}, []
    for name, v in arrays.items():
        v = np.ascontiguousarray(v)
        feeds[f"in_{name}"] = v
        args.append(nc.dram_tensor(f"in_{name}", v.shape, mb.dt.from_np(v.dtype), kind="ExternalInput").ap())
    args.append(nc.dram_tensor("out_0", (B, S, DM), mb.dt.float32, kind="ExternalOutput").ap())
    build(nc, *args)
    r = run_bass_kernel_spmd(nc, [feeds], core_ids=[0])
    return r.results[0]["out_0"]
```
